# Optimizing a Trainium2 kernel written in Bass

```python
import numpy as np
import jax
import jax.numpy as jnp

def _softmax(x, axis=-1):
    return jax.nn.softmax(x, axis=axis)

def _gelu(x):
    return jax.nn.gelu(x, approximate=True)

def _silu(x):
    return jax.nn.silu(x)

def _sigmoid(x):
    return jax.nn.sigmoid(x)

def _layernorm(x, axis=-1, eps=1e-05):
    m = jnp.mean(x, axis=axis, keepdims=True)
    v = jnp.var(x, axis=axis, keepdims=True)
    return (x - m) / jnp.sqrt(v + eps)

def _scatter_add(tgt, idx, src, axis=0):
    return tgt.at[idx].add(src)

def _segment_sum(src, seg, n):
    return jax.ops.segment_sum(src, seg, n)
kernel_name = 'mk_adj_preln_d1_adj_r2_a017d9'

def setup_inputs(seed: int=0):
    np.random.seed(seed)
    _w = jnp.asarray

    def _rec_inputs():
        import jax
        import jax.numpy as jnp
        _gk = jax.random.key(seed)
        x = -0.0002928 + 1 * jax.random.normal(jax.random.fold_in(_gk, 1), (8192, 256), jnp.float32)
        _w = (1.0 + jnp.arange(8192, dtype=jnp.float32)) ** (-0.5)
        _w = _w / _w.mean()
        _pij = jnp.clip(0.000244141 * _w[:, None] * _w[None, :], 0.0, 1.0)
        _a = jax.random.uniform(jax.random.fold_in(_gk, 2), (8192, 8192)) < _pij
        _a = jnp.logical_or(_a, jnp.eye(8192, dtype=bool))
        _af = _a.astype(jnp.float32)
        _af = _af * jax.random.uniform(jax.random.fold_in(_gk, 3), (8192, 8192), jnp.float32, 0.05, 1)
        adj = _af
        return (x, adj)
    x, adj = _rec_inputs()

    def _L0_gnn_setup():
        import jax, jax.numpy as jnp
        import numpy as np
        EPS = 1e-08
        key = jax.random.key(seed)
        k1, k2, k3, k4 = jax.random.split(key, 4)
        N, IN, OUT = (4096, 256, 256)
        x = jax.random.normal(k1, (N, IN), dtype=jnp.float32)
        adj = jax.random.uniform(k2, (N, N), dtype=jnp.float32)
        W = jax.random.normal(k3, (OUT, IN), dtype=jnp.float32) * (1.0 / np.sqrt(IN))
        b = jax.random.normal(k4, (OUT,), dtype=jnp.float32) * 0.01
        return {'x': x, 'adj': adj, 'W': W, 'b': b}
    _L0_gnn_all = _L0_gnn_setup()
    _L0_gnn_in = {k: v for k, v in _L0_gnn_all.items() if k in ('W', 'b')}
    del _L0_gnn_all
    return {'x': x, 'adj': adj, 'L0_gnn_W': _L0_gnn_in['W'], 'L0_gnn_b': _L0_gnn_in['b']}

def reference(x, adj, L0_gnn_W, L0_gnn_b):
    import jax
    import jax.numpy as jnp

    def _L0_gnn_ref(x, adj, W, b):
        import jax, jax.numpy as jnp
        import numpy as np
        EPS = 1e-08
        deg = adj.sum(axis=1)
        dis = (deg + EPS) ** (-0.5)
        a_norm = dis[:, None] * adj * dis[None, :]
        h = a_norm @ x
        return h @ W.T + b
    h = jnp.maximum(_layernorm(x, axis=-1), 0.0)
    x = x + _L0_gnn_ref(h, adj, L0_gnn_W, L0_gnn_b)
    return x

_drawn_inputs = setup_inputs


def setup_inputs(seed=0):
    import zlib

    import numpy as np

    out = dict(_drawn_inputs(seed))
    spreads = {}
    factors = {'L0_gnn_b': 7.393}
    for name, (base, spread) in spreads.items():
        noise = np.random.default_rng([zlib.crc32(name.encode()), seed]).standard_normal(out[name].shape)
        drawn = base * np.exp(spread * noise) if base else spread * noise
        out[name] = jnp.asarray(drawn.astype(out[name].dtype))
    for name, factor in factors.items():
        out[name] = (out[name] * factor).astype(out[name].dtype)
    return out
```

```python
from contextlib import ExitStack

import concourse.bass as bass
from concourse import mybir

F32 = mybir.dt.float32
F32R = mybir.dt.float32r
ALU = mybir.AluOpType
ACT = mybir.ActivationFunctionType
AX_X = mybir.AxisListType.X

LN_EPS = 1e-5
DEG_EPS = 1e-8


def gnn_block_kernel(nc, x, adj, W, b, out, part_dram):
    N, FD = x.shape
    T = 128
    S = 4
    UC = 1024
    NC = N // UC
    HC = UC // (4 * T)
    G = S * HC
    NQ = N // (S * T)
    QP = NQ // NC
    FH = FD // T
    NB = N // T
    assert HC == 2 and QP == 2 and FH == 2 and NC == 8

    L_UNITS = QP * NC * (NC - 1) // 2

    def counted(eng, name, start):
        reg = eng.alloc_register(name)
        eng.reg_mov(reg, start)
        return reg

    LAST_UNIT = L_UNITS + QP * NC * (NC + 1) // 2 - 1

    adj_rows = adj.rearrange("(r p) c -> p r c", p=T)
    x_rows = x.rearrange("(r p) f -> p r f", p=T)
    out_rows = out.rearrange("(r p) f -> p r f", p=T)

    with ExitStack() as ctx:
        def sb(name, shape, dt=F32):
            return ctx.enter_context(nc.sbuf_tensor(name, shape, dt))

        def pb(name, shape):
            return ctx.enter_context(nc.psum_tensor(name, shape, F32))

        def sem(name):
            return ctx.enter_context(nc.semaphore(name))

        hs = sb("hs", [T, NB, 2 * FD], F32R)
        mt = sb("mt", [T, S, UC])
        dt_ = sb("dt_", [T, S, UC])
        hi = sb("hi", [T, 4, 4 * T], F32R)
        lo = sb("lo", [T, 4, 4 * T], F32R)
        degp = sb("degp", [T, S * NC])
        xh = sb("xh", [T, S, FD])
        part = sb("part", [T, S, FD])
        tot = sb("tot", [T, S, FD])
        xb = sb("xb", [T, S, FD])
        b_bc = sb("b_bc", [T, FD])
        w_sb = sb("w_sb", [T, FH, FD])
        wT = sb("wT", [T, FH, FD])
        totT = sb("totT", [T, FH, T])
        ident = sb("ident", [T, T])
        stats = sb("stats", [T, S, 6])
        mv = sb("mv", [T, S, 2])
        sq = sb("sq", [T, 2, S])
        mhalf = sb("mhalf", [T, 2, S])
        rs = sb("rs", [T, 2, S])
        sc = sb("sc", [T, S])
        dis = sb("dis", [T, (NQ + 1) * S])
        zeros = sb("zeros", [T, T], F32R)

        acc = [pb(f"acc{s}", [T, 512]) for s in range(S)]
        at = [pb(f"at{i}", [T, 4 * T]) for i in range(2)]
        fin_t = pb("fin_t", [T, 512])
        fin_o = pb("fin_o", [T, 512])

        m_loaded = [sem(f"m_loaded{s}") for s in range(S)]
        d_loaded = [sem(f"d_loaded{s}") for s in range(2)]
        at_ready = sem("at_ready")
        hi_ready = sem("hi_ready")
        lo_ready = sem("lo_ready")
        pieces_used = sem("pieces_used")
        m_summed = sem("m_summed")
        d_summed = sem("d_summed")
        half_read = sem("half_read")
        acc_read = sem("acc_read")
        xh_loaded = sem("xh_loaded")
        z_ready = sem("z_ready")
        relu_done = sem("relu_done")
        hs_ready = sem("hs_ready")
        sq_ready = sem("sq_ready")
        rs_ready = sem("rs_ready")
        stats_done = sem("stats_done")
        mv_done = sem("mv_done")
        deg_done = sem("deg_done")
        sc_done = sem("sc_done")
        dis_done = sem("dis_done")
        part_stored = sem("part_stored")
        zero_stored = sem("zero_stored")
        tot_loaded = sem("tot_loaded")
        tot_used = sem("tot_used")
        totT_ready = sem("totT_ready")
        fin_ready = sem("fin_ready")
        xb_loaded = sem("xb_loaded")
        xb_ready = sem("xb_ready")
        o_ready = sem("o_ready")
        o_stored = sem("o_stored")
        w_loaded = sem("w_loaded")
        b_loaded = sem("b_loaded")
        wT_psum = sem("wT_psum")
        wT_ready = sem("wT_ready")
        zeros_ready = sem("zeros_ready")
        part_zero = sem("part_zero")
        ident_ready = sem("ident_ready")
        mhalf_ready = sem("mhalf_ready")

        block = ctx.enter_context(nc.Block())

        @block.sync
        def _(sp):
            def load_m(R, c, u1, s, summed=True):
                src = adj_rows[:, bass.ds(R * S + s, 1), bass.ds(c * UC, UC)]
                sp.compute_val(src.offset * 4)
                if u1 is not None:
                    transposed = sp.compute_val(u1 * G + HC * (s + 1))
                    sums = sp.compute_val(u1 * S + (s + 1))
                    sp.wait_ge(at_ready, transposed)
                    if summed:
                        sp.wait_ge(m_summed, sums)
                sp.dma_start(mt[:, s:s + 1, :], src
                             ).then_inc(m_loaded[s], 16)

            def load_d(R, c, d1, pair):
                src = adj_rows[:, bass.ds(R * S + 2 * pair, 2), bass.ds(c * UC, UC)]
                sp.compute_val(src.offset * 4)
                if d1 is not None:
                    sp.wait_ge(d_summed, d1 * S + 2 * (pair + 1))
                sp.dma_start(dt_[:, 2 * pair:2 * pair + 2, :],
                             src
                             ).then_inc(d_loaded[pair], 16)

            def both(R, i, u1, d1):
                for pair in range(2):
                    load_m(R, i, u1, 2 * pair)
                    load_m(R, i, u1, 2 * pair + 1)
                    load_d(R, NC - 1 - i, d1, pair)

            def only_d(R, i, d1):
                for pair in range(2):
                    load_d(R, NC - 1 - i, d1, pair)

            def only_m(R, c, u1, summed=True):
                for s in range(S):
                    load_m(R, c, u1, s, summed)

            u_reg = counted(sp, "sp_u", 1)
            d_reg = counted(sp, "sp_d", 0)

            def loop_both(R, first, end):
                with sp.Fori(first, end) as i:
                    both(R, i, sp.snap(u_reg), sp.snap(d_reg))
                    sp.reg_add(u_reg, u_reg, 1)
                    sp.reg_add(d_reg, d_reg, 1)

            def loop_only_d(R, first, end):
                with sp.Fori(first, end) as i:
                    only_d(R, i, sp.snap(d_reg))
                    sp.reg_add(d_reg, d_reg, 1)

            def loop_only_m(R, first, end, summed=True):
                with sp.Fori(first, end) as c:
                    only_m(R, c, sp.snap(u_reg), summed)
                    sp.reg_add(u_reg, u_reg, 1)

            only_d(0, 0, None)
            loop_only_d(0, 1, NC)
            loop_only_d(1, 0, NC)
            for h in range(QP):
                both(QP + h, 0, None if h == 0 else 0, sp.snap(d_reg))
                sp.reg_add(d_reg, d_reg, 1)
                loop_only_d(QP + h, 1, NC - 1)
            with sp.Fori(2, NC // 2) as P:
                with sp.Fori(0, QP) as h:
                    loop_both(P * QP + h, 0, P)
                    loop_only_d(P * QP + h, P, NC - P)
            with sp.Fori(0, QP) as h:
                loop_both(NC // 2 * QP + h, 0, NC // 2)
            with sp.Fori(NC // 2 + 1, NC) as P:
                with sp.Fori(0, QP) as h:
                    loop_both(P * QP + h, 0, NC - P)
                    loop_only_m(P * QP + h, NC - P, P)
            only_m(NQ - 1, NC - 1, L_UNITS - 1)
            sp.reg_mov(u_reg, L_UNITS)
            with sp.Fori(0, NC - 1) as P:
                with sp.Fori(0, QP) as h:
                    loop_only_m(P * QP + h, P, NC, summed=False)
            only_m(NQ - 2, NC - 1, LAST_UNIT - 1, summed=False)

        @block.tensor
        def _(pe):
            def transposes(u, k):
                s, half = k // HC, k % HC
                if half == 0:
                    pe.wait_ge(m_loaded[s], (u + 1) * 16)
                for j in range(4):
                    col = (half * 4 + j) * T
                    last = pe.transpose(at[k % 2][:, j * T:(j + 1) * T], mt[:, s, col:col + T], ident[:, :])
                last.then_inc(at_ready, 1)

            def products(c, k):
                s, half = k // HC, k % HC
                for j in range(4):
                    jb = c * (UC // T) + (half * 4 + j)
                    at_hi = hi[:, k % 4, j * T:(j + 1) * T]
                    at_lo = lo[:, k % 4, j * T:(j + 1) * T]
                    pe.matmul(acc[s][:, :], at_hi, hs[:, bass.ds(jb, 1), :],
                              start=False, stop=True, skip_group_check=True)
                    last = pe.matmul(acc[s][:, 0:FD], at_lo, hs[:, bass.ds(jb, 1), 0:FD],
                                     start=False, stop=True, skip_group_check=True)
                last.then_inc(pieces_used, 1)

            def clear(Q, s):
                if not (isinstance(Q, int) and Q == 0):
                    pe.wait_ge(acc_read, (Q - 1) * S + s + 1)
                pe.matmul(acc[s][:, 0:2], zeros[:, :], zeros[:, 0:2], start=True, stop=True, skip_group_check=True)

            def turn_total(n, s):
                pe.wait_ge(acc_read, (NQ - QP + n) * S + s + 1)
                for f in range(FH):
                    last = pe.transpose(fin_t[:, f * T:(f + 1) * T], tot[:, s, f * T:(f + 1) * T], ident[:, :])
                last.then_inc(tot_used, 1)

            def times_w(n, s):
                pe.wait_ge(totT_ready, n * S + s + 1)
                if not (isinstance(n, int) and n == 0 and s == 0):
                    pe.wait_ge(o_ready, n * S + s)
                for f in range(FH):
                    last = pe.matmul(fin_o[:, 0:FD], totT[:, f, :], wT[:, f, :], start=(f == 0), stop=(f == FH - 1))
                last.then_inc(fin_ready, 1)

            def unit(u, c, quad=None, finish=None, ends=False, phase1=False):
                if phase1:
                    pe.wait_ge(hs_ready, (c + 1) * QP)
                for k in range(G):
                    pe.wait_ge(lo_ready, u * G + (k + 1))
                    if k + 2 < G:
                        transposes(u, k + 2)
                    elif not ends:
                        transposes(u + 1, k + 2 - G)
                    if quad is not None and k % HC == 0:
                        clear(quad, k // HC)
                    products(c, k)
                    if finish is not None:
                        if 2 <= k <= 5:
                            times_w(finish, k - 2)
                        if 1 <= k <= 4:
                            turn_total(finish, k - 1)

            pe.wait_ge(ident_ready, 2)
            pe.wait_ge(zeros_ready, 1)
            pe.wait_ge(w_loaded, 16)
            for f in range(FH):
                for o in range(FH):
                    last = pe.transpose(fin_t[:, (f * FH + o) * T:(f * FH + o + 1) * T],
                                        w_sb[:, o, f * T:(f + 1) * T], ident[:, :])
            last.then_inc(wT_psum, 1)
            pe.wait_ge(wT_ready, 1)

            transposes(0, 0)
            transposes(0, 1)
            for h in range(QP):
                unit(h, 0, quad=h, phase1=True)
            u_reg = counted(pe, "pe_u", QP)

            def loop_unit(first, end, phase1=False):
                with pe.Fori(first, end) as c:
                    unit(pe.snap(u_reg), c, phase1=phase1)
                    pe.reg_add(u_reg, u_reg, 1)

            with pe.Fori(2, NC) as P:
                with pe.Fori(0, QP) as h:
                    unit(pe.snap(u_reg), 0, quad=P * QP + h - QP, phase1=True)
                    pe.reg_add(u_reg, u_reg, 1)
                    loop_unit(1, P, phase1=True)
            pe.wait_ge(hs_ready, NQ)
            unit(L_UNITS, NC - 1, quad=NQ - QP)
            pe.reg_mov(u_reg, L_UNITS + 1)
            with pe.Fori(0, NC - 1) as P:
                with pe.Fori(0, QP) as h:
                    unit(pe.snap(u_reg), P, quad=P * QP + h + (NQ - QP + 1), finish=P * QP + h)
                    pe.reg_add(u_reg, u_reg, 1)
                    loop_unit(P + 1, NC)
            unit(LAST_UNIT, NC - 1, quad=2 * NQ - QP - 1, finish=NQ - 2, ends=True)
            for s in range(S):
                turn_total(NQ - 1, s)
                times_w(NQ - 1, s)

        @block.scalar
        def _(act):
            def upper(u, k):
                g = u * G + k
                act.wait_ge(at_ready, g + 1)
                if not (isinstance(u, int) and u == 0 and k < 4):
                    act.wait_ge(pieces_used, g - 3)
                nc.scalar.activation(hi[:, k % 4, :], at[k % 2][:, :], ACT.Copy).then_inc(hi_ready, 1)

            def sum_d(R, i, d, s):
                if s % 2 == 0:
                    act.wait_ge(d_loaded[s // 2], (d + 1) * 16)
                nc.scalar.activation(dt_[:, s, :], dt_[:, s, :], ACT.Copy,
                                     accum_out=degp[:, bass.ds(s * NC + (NC - 1) - i, 1)]).then_inc(d_summed, 1)

            def relu(R):
                act.wait_ge(z_ready, (R + 1) * S)
                nc.scalar.activation(hs[:, bass.ds(R * S, S), 0:FD], xh[:, :, :], ACT.Relu).then_inc(relu_done, 1)

            def copy_total(n, s):
                act.wait_ge(tot_used, n * S + s + 1)
                if not (isinstance(n, int) and n == 0 and s == 0):
                    act.wait_ge(fin_ready, n * S + s)
                nc.scalar.activation(totT[:, :, :], fin_t[:, 0:FD], ACT.Copy).then_inc(totT_ready, 1)

            def both(R, i, u, d):
                for s in range(S):
                    for k in range(HC * s, HC * (s + 1)):
                        upper(u, k)
                    sum_d(R, i, d, s)

            def only_m(u, finish=None):
                for k in range(G):
                    upper(u, k)
                    if finish is not None and 3 <= k <= 6:
                        copy_total(finish, k - 3)

            u_reg = counted(act, "act_u", QP)
            d_reg = counted(act, "act_d", 0)

            def loop_both(R, first, end):
                with act.Fori(first, end) as i:
                    both(R, i, act.snap(u_reg), act.snap(d_reg))
                    act.reg_add(u_reg, u_reg, 1)
                    act.reg_add(d_reg, d_reg, 1)

            def loop_only_d(R, first, end):
                with act.Fori(first, end) as i:
                    for s in range(S):
                        sum_d(R, i, act.snap(d_reg), s)
                    act.reg_add(d_reg, d_reg, 1)

            def loop_only_m(first, end):
                with act.Fori(first, end) as i:
                    only_m(act.snap(u_reg))
                    act.reg_add(u_reg, u_reg, 1)

            act.wait_ge(wT_psum, 1)
            nc.scalar.activation(wT[:, :, :], fin_t[:, :], ACT.Copy).then_inc(wT_ready, 1)
            for h in range(QP):
                loop_only_d(h, 0, NC)
                relu(h)
            for h in range(QP):
                both(QP + h, 0, h, act.snap(d_reg))
                act.reg_add(d_reg, d_reg, 1)
                loop_only_d(QP + h, 1, NC - 1)
                relu(QP + h)
            with act.Fori(2, NC // 2) as P:
                with act.Fori(0, QP) as h:
                    loop_both(P * QP + h, 0, P)
                    loop_only_d(P * QP + h, P, NC - P)
                    relu(P * QP + h)
            with act.Fori(0, QP) as h:
                loop_both(NC // 2 * QP + h, 0, NC // 2)
                relu(NC // 2 * QP + h)
            with act.Fori(NC // 2 + 1, NC) as P:
                with act.Fori(0, QP) as h:
                    loop_both(P * QP + h, 0, NC - P)
                    loop_only_m(NC - P, P)
                    relu(P * QP + h)
            only_m(L_UNITS)
            act.reg_mov(u_reg, L_UNITS + 1)
            with act.Fori(0, NC - 1) as P:
                with act.Fori(0, QP) as h:
                    only_m(act.snap(u_reg), finish=P * QP + h)
                    act.reg_add(u_reg, u_reg, 1)
                    loop_only_m(P + 1, NC)
            only_m(LAST_UNIT, finish=NQ - 2)
            for s in range(S):
                copy_total(NQ - 1, s)

        @block.vector
        def _(dve):
            def lower(u, k):
                dve.wait_ge(hi_ready, u * G + (k + 1))
                nc.vector.tensor_tensor(lo[:, k % 4, :], at[k % 2][:, :], hi[:, k % 4, :].bitcast(F32),
                                        ALU.subtract).then_inc(lo_ready, 1)

            def sum_m(R, c, u, s):
                nc.vector.tensor_reduce(degp[:, bass.ds(s * NC + c, 1)], mt[:, s, :], AX_X, ALU.add
                                        ).then_inc(m_summed, 1)

            def read_acc(Q, u, s, dst, other):
                dve.wait_ge(pieces_used, u * G + HC * (s + 1))
                if other is None:
                    step = nc.vector.tensor_copy(dst, acc[s][:, FD:2 * FD])
                else:
                    step = nc.vector.tensor_tensor(dst, acc[s][:, FD:2 * FD], other, ALU.add)
                step.then_inc(half_read, 1)
                dve.wait_ge(half_read, Q * S + s + 1)
                nc.vector.tensor_tensor(dst, acc[s][:, 0:FD], dst, ALU.add).then_inc(acc_read, 1)

            def spill(e, u, s):
                if not (isinstance(e, int) and e == 0):
                    dve.wait_ge(part_stored, e * 16)
                if s == 0:
                    dve.wait_ge(part_zero, 1)
                    dve.wait_ge(zero_stored, 16 * QP)
                read_acc(e, u, s, part[:, s, :], None)

            def full(n, u, s):
                dve.wait_ge(tot_loaded, (n + 1) * 16)
                read_acc(NQ - QP + n, u, s, tot[:, s, :], tot[:, s, :])

            def output(n, s):
                dve.wait_ge(fin_ready, n * S + s + 1)
                dve.wait_ge(xb_ready, n + 1)
                nc.vector.scalar_tensor_tensor(out=xb[:, s, :], in0=fin_o[:, 0:FD],
                                               scalar=dis[:, bass.ds(n * S + s, 1)], in1=xb[:, s, :],
                                               op0=ALU.mult, op1=ALU.add).then_inc(o_ready, 1)

            def build_h(R, d, u):
                dve.wait_ge(xh_loaded, (R + 1) * 16)
                for s in range(S):
                    nc.vector.bn_stats(stats[:, s, :], xh[:, s, :]).then_inc(stats_done, 1)
                dve.wait_ge(stats_done, (R + 1) * S)
                dve.wait_ge(d_summed, d * S)
                if u is not None:
                    dve.wait_ge(m_summed, u * S)
                nc.vector.tensor_reduce(sq[:, 1, :], degp[:, :].rearrange("p (s c) -> p s c", s=S), AX_X, ALU.add
                                        ).then_inc(deg_done, 1)
                for s in range(S):
                    nc.vector.bn_aggr(mv[:, s, :], stats[:, s, :]).then_inc(mv_done, 1)
                dve.wait_ge(mv_done, (R + 1) * S)
                nc.vector.tensor_scalar(sq[:, 0, :], mv[:, :, 1], LN_EPS, None, ALU.add).then_inc(sq_ready, 1)
                dve.wait_ge(deg_done, R + 1)
                nc.vector.tensor_scalar(sq[:, 1, :], sq[:, 1, :], DEG_EPS, None, ALU.add).then_inc(sq_ready, 1)
                dve.wait_ge(rs_ready, R + 1)
                nc.vector.tensor_tensor(sc[:, :], rs[:, 0, :], rs[:, 1, :], ALU.mult).then_inc(sc_done, 1)
                nc.vector.tensor_copy(dis[:, bass.ds((R + 1) * S, S)], rs[:, 1, :]).then_inc(dis_done, 1)
                dve.wait_ge(sc_done, R + 1)
                for s in range(S):
                    nc.vector.tensor_scalar(xh[:, s, :], xh[:, s, :], mv[:, s, 0:1], sc[:, s:s + 1],
                                            ALU.subtract, ALU.mult).then_inc(z_ready, 1)
                dve.wait_ge(relu_done, R + 1)
                nc.vector.scalar_tensor_tensor(out=hs[:, bass.ds(R * S, S), FD:2 * FD], in0=xh[:, :, :], scalar=0.0,
                                               in1=hs[:, bass.ds(R * S, S), 0:FD].bitcast(F32),
                                               op0=ALU.max, op1=ALU.subtract).then_inc(hs_ready, 1)

            READ_AT = [0, 1, 2, 4]

            def unit(u, R=None, c=None, spilled=None, finish=None):
                for k in range(G):
                    if k in READ_AT:
                        s = READ_AT.index(k)
                        if spilled is not None:
                            spill(spilled, u - 1, s)
                        if finish is not None:
                            full(finish, u - 1, s)
                    lower(u, k)
                    if R is not None and k % HC == HC - 1:
                        sum_m(R, c, u, k // HC)
                    if finish is not None and k >= 4:
                        output(finish, k - 4)

            u_reg = counted(dve, "dve_u", QP)
            d_reg = counted(dve, "dve_d", QP * (2 * NC - 1))

            def loop_unit(first, end, R=None):
                with dve.Fori(first, end) as c:
                    unit(dve.snap(u_reg), R, c)
                    dve.reg_add(u_reg, u_reg, 1)

            for h in range(QP):
                build_h(h, NC * (h + 1), None)
            for h in range(QP):
                unit(h, QP + h, 0, spilled=0 if h else None)
                build_h(QP + h, QP * NC + (NC - 1) * (h + 1), h + 1)
            with dve.Fori(2, NC) as P:
                with dve.Fori(0, QP) as h:
                    R = P * QP + h
                    unit(dve.snap(u_reg), R, 0, spilled=R - QP - 1)
                    dve.reg_add(u_reg, u_reg, 1)
                    loop_unit(1, P, R)
                    with dve.Fori(P, NC) as i:
                        dve.reg_add(d_reg, d_reg, 1)
                    build_h(R, dve.snap(d_reg), dve.snap(u_reg))
            dve.wait_ge(dis_done, NQ)
            nc.vector.tensor_copy(dis[:, 0:S], dis[:, NQ * S:(NQ + 1) * S]).then_inc(dis_done, 1)
            unit(L_UNITS, spilled=NQ - QP - 1)
            dve.wait_ge(dis_done, NQ + 1)
            dve.reg_mov(u_reg, L_UNITS + 1)
            with dve.Fori(0, NC - 1) as P:
                with dve.Fori(0, QP) as h:
                    unit(dve.snap(u_reg), finish=P * QP + h)
                    dve.reg_add(u_reg, u_reg, 1)
                    loop_unit(P + 1, NC)
            unit(LAST_UNIT, finish=NQ - 2)
            for s in range(S):
                full(NQ - 1, LAST_UNIT, s)
                output(NQ - 1, s)

        @block.gpsimd
        def _(pool):
            def load_xh(R):
                if not (isinstance(R, int) and R == 0):
                    pool.wait_ge(hs_ready, R)
                pool.dma_start(xh[:, :, :], x_rows[:, bass.ds(R * S, S), :]).then_inc(xh_loaded, 16)

            def power(R):
                pool.wait_ge(sq_ready, (R + 1) * 2)
                nc.gpsimd.tensor_tensor(rs[:, :, :], sq[:, :, :], mhalf[:, :, :], ALU.pow).then_inc(rs_ready, 1)

            def store_part(R):
                pool.wait_ge(acc_read, (R - QP + 1) * S)
                pool.dma_start(part_dram[:, bass.ds(R * S, S), :], part[:, :, :]).then_inc(part_stored, 16)

            def load_last(n, R):
                if not (isinstance(n, int) and n == 0):
                    pool.wait_ge(tot_used, n * S)
                    pool.wait_ge(o_stored, n * 16)
                pool.dma_start(tot[:, :, :], part_dram[:, bass.ds(R * S, S), :]).then_inc(tot_loaded, 16)
                pool.dma_start(xb[:, :, :], x_rows[:, bass.ds(R * S, S), :]).then_inc(xb_loaded, 16)
                pool.wait_ge(xb_loaded, (n + 1) * 16)
                nc.gpsimd.tensor_tensor(xb[:, :, :], xb[:, :, :],
                                        b_bc[:, :].rearrange("p (s f) -> p s f", s=1).to_broadcast([T, S, FD]),
                                        ALU.add).then_inc(xb_ready, 1)

            def store_out(n, R):
                pool.wait_ge(o_ready, (n + 1) * S)
                if isinstance(R, int):
                    rows = R * S
                else:
                    pool.reg_add(out_reg, out_reg, S)
                    rows = pool.snap(out_reg, min_val=S, max_val=(NQ - 1) * S) - S
                pool.dma_start(out_rows[:, bass.ds(rows, S), :], xb[:, :, :]).then_inc(o_stored, 16)

            load_xh(0)
            pool.dma_start(w_sb[:, :, :], W.rearrange("(q p) f -> p q f", p=T)).then_inc(w_loaded, 16)
            pool.dma_start(b_bc[:, :], b.partition_broadcast(T)).then_inc(b_loaded, 16)
            nc.gpsimd.memset(mhalf[:, :, :], -0.5).then_inc(mhalf_ready, 1)
            nc.gpsimd.memset(zeros[:, :].bitcast(F32), 0.0).then_inc(zeros_ready, 1)
            nc.gpsimd.memset(ident[:, :], 0.0).then_inc(ident_ready, 1)
            nc.gpsimd.memset(part[:, :, :], 0.0).then_inc(part_zero, 1)
            pool.wait_ge(ident_ready, 1)
            nc.gpsimd.affine_select(out=ident[:, :], in_=ident[:, :], compare_op=ALU.not_equal, fill=1.0, base=0,
                                    pattern=[[-1, T]], channel_multiplier=1).then_inc(ident_ready, 1)
            pool.wait_ge(part_zero, 1)
            for R in range(QP):
                pool.dma_start(part_dram[:, R * S:(R + 1) * S, :], part[:, :, :]).then_inc(zero_stored, 16)
            pool.wait_ge(mhalf_ready, 1)
            for R in range(QP + 1):
                if R > 0:
                    load_xh(R)
                power(R)
            load_xh(QP + 1)
            with pool.Fori(QP + 1, NQ - 1) as R:
                store_part(R - 1)
                power(R)
                load_xh(R + 1)
            store_part(NQ - 2)
            power(NQ - 1)
            store_part(NQ - 1)
            pool.wait_ge(part_stored, 16 * (NQ - QP))
            pool.wait_ge(zero_stored, 16 * QP)
            pool.wait_ge(b_loaded, 16)
            load_last(0, NQ - 1)
            store_out(0, NQ - 1)
            out_reg = counted(pool, "pool_out", 0)
            with pool.Fori(0, NQ - 1) as R:
                load_last(R + 1, R)
                store_out(R + 1, R)
            pool.wait_ge(o_stored, 16 * NQ)


_INS = ["x", "adj", "L0_gnn_W", "L0_gnn_b"]


def kernel(**inputs):
    import numpy as _np
    import concourse.bacc as _bacc
    from concourse import mybir as _mybir
    from concourse.bass_utils import run_bass_kernel_spmd as _run

    nc = _bacc.Bacc("TRN2", target_bir_lowering=False, num_devices=1)
    arrays, args = {}, []
    for name in _INS:
        a = _np.ascontiguousarray(inputs[name])
        arrays[f"in_{name}_dram"] = a
        args.append(nc.dram_tensor(f"in_{name}_dram", a.shape, _mybir.dt.from_np(a.dtype), kind="ExternalInput").ap())
    shape = inputs["x"].shape
    out = nc.dram_tensor("out_0_dram", shape, _mybir.dt.float32, kind="ExternalOutput").ap()
    part = nc.dram_tensor("part_dram", (128, shape[0] // 128, shape[1]), _mybir.dt.float32, kind="Internal").ap()
    gnn_block_kernel(nc, *args, out, part)
    r = _run(nc, [arrays], core_ids=[0])
    return r.results[0]["out_0_dram"]
```

```python
from contextlib import ExitStack

import concourse.bass as bass
from concourse import mybir

F32 = mybir.dt.float32
F32R = mybir.dt.float32r
ALU = mybir.AluOpType
ACT = mybir.ActivationFunctionType
AX_X = mybir.AxisListType.X

LN_EPS = 1e-5
DEG_EPS = 1e-8


def gnn_block_kernel(nc, x, adj, W, b, out, part_dram):
    N, FD = x.shape
    T = 128
    B = 32
    Q = T // B
    S = 4
    V = 2
    UC = 1024
    RUN = UC // Q
    M = UC // T
    NC = N // UC
    HC = 2
    G = S * HC
    NQ = N // (S * T)
    QP = NQ // NC
    FH = FD // T
    ACT_SUMS = 3
    assert QP == 2 and FH == 2 and NC == 8 and M == HC * 4

    L_UNITS = QP * NC * (NC - 1) // 2
    UNITS = L_UNITS + QP * NC * (NC + 1) // 2
    L_TURNS = NQ - QP
    FIRST_M = NC
    D_UNITS = NC + QP * NC * (NC - 1) // 2

    def counted(eng, name, start):
        reg = eng.alloc_register(name)
        eng.reg_mov(reg, start)
        return reg

    adj_rows = adj.rearrange("(r p) c -> p r c", p=T)
    adj_blocks = adj.rearrange("(r i) (c a l) -> a i r c l", i=B, a=Q, l=RUN)
    x_rows = x.rearrange("(r p) f -> p r f", p=T)
    x_cols = x.rearrange("(c a m j) f -> c a j m f", a=Q, m=M, j=B)
    out_rows = out.rearrange("(r p) f -> p r f", p=T)

    with ExitStack() as ctx:
        def sb(name, shape, dt=F32):
            return ctx.enter_context(nc.sbuf_tensor(name, shape, dt))

        def pb(name, shape):
            return ctx.enter_context(nc.psum_tensor(name, shape, F32))

        def sem(name):
            return ctx.enter_context(nc.semaphore(name))

        hs = sb("hs", [T, NC * M, 2 * FD], F32R)
        mt = sb("mt", [T, S, UC])
        dt_ = sb("dt_", [T, S, UC])
        tt = sb("tt", [T, 2, UC])
        hi = sb("hi", [T, 4, 4 * T], F32R)
        lo = sb("lo", [T, 4, 4 * T], F32R)
        lsum = sb("lsum", [T, QP, S * Q * NC])
        dsum = sb("dsum", [T, QP, S * NC])
        z = sb("z", [T, QP, S * Q])
        dq = sb("dq", [T, QP, S])
        nx = sb("nx", [T, M, FD])
        part = sb("part", [T, S, FD])
        b_bc = sb("b_bc", [T, FD])
        w_sb = sb("w_sb", [T, FH, FD])
        wT = sb("wT", [T, FH, FD])
        totT = sb("totT", [T, FH, T])
        ident = sb("ident", [T, T])
        same = sb("same", [T, T])
        zeros = sb("zeros", [T, T], F32R)
        stats = sb("stats", [T, M, 6])
        mv = sb("mv", [T, M, 2])
        vare = sb("vare", [T, M])
        rstd = sb("rstd", [T, M])
        dege = sb("dege", [T, QP * S * Q])
        disq = sb("disq", [T, QP * S * Q])
        mhalf = sb("mhalf", [T, QP * S * Q])
        disx = sb("disx", [T, M])
        dis = sb("dis", [T, NQ * S])
        tot = dt_[:, 0, :].rearrange("p (s f) -> p s f", s=S)
        xb = dt_[:, 1, :].rearrange("p (s f) -> p s f", s=S)
        res = dt_[:, 2, :].rearrange("p (s f) -> p s f", s=S)

        acc = [pb(f"acc{s}", [T, 512]) for s in range(S)]
        fin_t = pb("fin_t", [T, 512])
        fin_o = pb("fin_o", [T, 512])
        deg_ps = pb("deg_ps", [T, 512])

        m_loaded = [sem(f"m_loaded{v}") for v in range(S // V)]
        p0_loaded = [sem(f"p0_loaded{s}") for s in range(S)]
        d_loaded = [sem(f"d_loaded{s}") for s in range(S)]
        tt_ready = sem("tt_ready")
        hi_ready = sem("hi_ready")
        lo_ready = sem("lo_ready")
        pieces_used = sem("pieces_used")
        m_summed = sem("m_summed")
        m_summed_dve = sem("m_summed_dve")
        p0_summed = sem("p0_summed")
        d_summed = sem("d_summed")
        quad_summed = sem("quad_summed")
        dsum_clear = sem("dsum_clear")
        z_ready = sem("z_ready")
        spread_ready = sem("spread_ready")
        dege_ready = sem("dege_ready")
        disq_ready = sem("disq_ready")
        disx_ready = sem("disx_ready")
        dis_ready = sem("dis_ready")
        nx_loaded = sem("nx_loaded")
        stats_done = sem("stats_done")
        mv_done = sem("mv_done")
        vare_ready = sem("vare_ready")
        rstd_ready = sem("rstd_ready")
        nx_scaled = sem("nx_scaled")
        nx_ready = sem("nx_ready")
        hs_hi = sem("hs_hi")
        hs_ready = sem("hs_ready")
        acc_read = sem("acc_read")
        part_stored = sem("part_stored")
        zero_stored = sem("zero_stored")
        tot_loaded = sem("tot_loaded")
        tot_used = sem("tot_used")
        totT_ready = sem("totT_ready")
        fin_ready = sem("fin_ready")
        xb_loaded = sem("xb_loaded")
        xb_ready = sem("xb_ready")
        res_ready = sem("res_ready")
        o_ready = sem("o_ready")
        o_stored = sem("o_stored")
        w_loaded = sem("w_loaded")
        b_loaded = sem("b_loaded")
        wT_psum = sem("wT_psum")
        wT_ready = sem("wT_ready")
        ident_ready = sem("ident_ready")
        same_ready = sem("same_ready")
        fills_ready = sem("fills_ready")

        SAME_STEPS = 2 * Q
        FILLS = 5

        block = ctx.enter_context(nc.Block())

        @block.sync
        def _(sp):
            def load_p0(R, c, t, s):
                if t > 0:
                    sp.wait_ge(p0_summed, (t - 1) * S + s + 1)
                sp.dma_start(mt[:, s, :], adj_rows[:, R * S + s, c * UC:(c + 1) * UC]).then_inc(p0_loaded[s], 16)

            def load_m(R, c, u1, v, summed=True):
                src = [adj_blocks[a, :, bass.ds((R * S + v * V) * Q, V * Q), bass.ds(c, 1), :] for a in range(Q)]
                for a in range(Q):
                    sp.compute_val(src[a].offset * 4)
                if u1 is None:
                    sp.wait_ge(p0_summed, (FIRST_M - 1) * S + (v + 1) * V)
                else:
                    turned = sp.compute_val(u1 * S + (v + 1) * V)
                    sums = sp.compute_val(u1 * ACT_SUMS + min((v + 1) * V, ACT_SUMS))
                    sums_dve = sp.compute_val(u1 + 1)
                    sp.wait_ge(tt_ready, turned)
                    if summed:
                        sp.wait_ge(m_summed, sums)
                        if v == 1:
                            sp.wait_ge(m_summed_dve, sums_dve)
                for a in range(Q):
                    sp.dma_start(mt[a * B:(a + 1) * B, v * V:(v + 1) * V, :].rearrange("i s (b l) -> i (s b) l", b=Q),
                                 src[a].rearrange("i r c l -> i (r c) l")).then_inc(m_loaded[v], 16)

            def load_d(R, c, d1, s):
                src = adj_rows[:, bass.ds(R * S + s, 1), bass.ds(c * UC, UC)]
                sp.compute_val(src.offset * 4)
                if d1 is not None:
                    sp.wait_ge(d_summed, d1 * S + (s + 1))
                sp.dma_start(dt_[:, s:s + 1, :], src).then_inc(d_loaded[s], 16)

            def both(R, i, u1, d1):
                for v in range(S // V):
                    load_m(R, i, u1, v)
                    for s in range(v * V, (v + 1) * V):
                        load_d(R, NC - 1 - i, d1, s)

            u_reg = counted(sp, "sp_u", 0)
            d_reg = counted(sp, "sp_d", NC - 1)

            def loop_both(R, first, end):
                with sp.Fori(first, end) as i:
                    both(R, i, sp.snap(u_reg), sp.snap(d_reg))
                    sp.reg_add(u_reg, u_reg, 1)
                    sp.reg_add(d_reg, d_reg, 1)

            def loop_only_d(R, first, end):
                with sp.Fori(first, end) as i:
                    for s in range(S):
                        load_d(R, NC - 1 - i, sp.snap(d_reg), s)
                    sp.reg_add(d_reg, d_reg, 1)

            def loop_only_m(R, first, end, summed=True):
                with sp.Fori(first, end) as c:
                    for v in range(S // V):
                        load_m(R, c, sp.snap(u_reg), v, summed)
                    sp.reg_add(u_reg, u_reg, 1)

            for R in range(QP):
                for i in range(NC // 2):
                    t = R * (NC // 2) + i
                    for s in range(S):
                        load_d(R, NC - 1 - i, t - 1 if t > 0 else None, s)
                        load_p0(R, i, t, s)
            both(QP, 0, None, NC - 1)
            sp.reg_add(d_reg, d_reg, 1)
            loop_only_d(QP, 1, NC - 1)
            loop_both(QP + 1, 0, 1)
            loop_only_d(QP + 1, 1, NC - 1)
            with sp.Fori(2, NC // 2) as P:
                with sp.Fori(0, QP) as h:
                    loop_both(P * QP + h, 0, P)
                    loop_only_d(P * QP + h, P, NC - P)
            with sp.Fori(0, QP) as h:
                loop_both(NC // 2 * QP + h, 0, NC // 2)
            with sp.Fori(NC // 2 + 1, NC) as P:
                with sp.Fori(0, QP) as h:
                    loop_both(P * QP + h, 0, NC - P)
                    loop_only_m(P * QP + h, NC - P, P)
            for v in range(S // V):
                load_m(0, 0, L_UNITS - 1, v)
            sp.reg_mov(u_reg, L_UNITS)
            loop_only_m(0, 1, NC, summed=False)
            loop_only_m(1, 0, NC, summed=False)
            with sp.Fori(1, NC) as P:
                with sp.Fori(0, QP) as h:
                    loop_only_m(P * QP + h, P, NC, summed=False)

        @block.tensor
        def _(pe):
            def products(u, c, k):
                s, half = k // HC, k % HC
                pe.wait_ge(lo_ready, u * G + (k + 1))
                for j in range(4):
                    tile = c * M + (half * 4 + j)
                    for half_h in (0, 1):
                        pe.matmul(acc[s][:, 0:FD], hi[:, k % 4, j * T:(j + 1) * T],
                                  hs[:, bass.ds(tile, 1), half_h * FD:(half_h + 1) * FD],
                                  start=False, stop=True, skip_group_check=True)
                    last = pe.matmul(acc[s][:, 0:FD], lo[:, k % 4, j * T:(j + 1) * T], hs[:, bass.ds(tile, 1), 0:FD],
                                     start=False, stop=True, skip_group_check=True)
                last.then_inc(pieces_used, 1)

            def clear(turn, s):
                if not (isinstance(turn, int) and turn == 0):
                    pe.wait_ge(acc_read, (turn - 1) * S + (s + 1))
                pe.matmul(acc[s][:, 0:2], zeros[:, :], zeros[:, 0:2], start=True, stop=True, skip_group_check=True)

            def spread(P):
                pe.wait_ge(z_ready, (P + 1) * (QP * Q))
                pe.matmul(deg_ps[:, 0:QP * S * Q], same[:, :], z[:, :, :], start=True, stop=True
                          ).then_inc(spread_ready, 1)

            def turn_total(n, s):
                pe.wait_ge(acc_read, (n + L_TURNS) * S + (s + 1))
                for f in range(FH):
                    last = pe.transpose(fin_t[:, f * T:(f + 1) * T], tot[:, s, f * T:(f + 1) * T], ident[:, :])
                last.then_inc(tot_used, 1)

            def times_w(n, s):
                pe.wait_ge(totT_ready, n * S + (s + 1))
                for f in range(FH):
                    last = pe.matmul(fin_o[:, 0:FD], totT[:, f, :], wT[:, f, :], start=(f == 0), stop=(f == FH - 1))
                last.then_inc(fin_ready, 1)

            def unit(u, c, turn=None, finish=None, spreads=None, new_h=False):
                if new_h:
                    pe.wait_ge(hs_ready, (c + 1) * M)
                for k in range(G):
                    if turn is not None and k % HC == 0:
                        clear(turn, k // HC)
                    products(u, c, k)
                    if spreads is not None and k == 0:
                        spread(spreads)
                    if finish is not None:
                        if 2 <= k <= 5:
                            times_w(finish, k - 2)
                        if 1 <= k <= 4:
                            turn_total(finish, k - 1)

            pe.wait_ge(ident_ready, 2)
            pe.wait_ge(same_ready, SAME_STEPS)
            pe.wait_ge(fills_ready, FILLS)
            pe.wait_ge(w_loaded, 16)
            for f in range(FH):
                for o in range(FH):
                    last = pe.transpose(fin_t[:, (f * FH + o) * T:(f * FH + o + 1) * T],
                                        w_sb[:, o, f * T:(f + 1) * T], ident[:, :])
            last.then_inc(wT_psum, 1)
            pe.wait_ge(wT_ready, 1)

            spread(0)
            for h in range(QP):
                unit(h, 0, turn=h, new_h=True)
            u_reg = counted(pe, "pe_u", QP)

            def next_unit(c, **kw):
                unit(pe.snap(u_reg), c, **kw)
                pe.reg_add(u_reg, u_reg, 1)

            def loop_units(first, end, new_h=False):
                with pe.Fori(first, end) as c:
                    next_unit(c, new_h=new_h)

            with pe.Fori(2, NC) as P:
                for h in range(QP):
                    next_unit(0, turn=P * QP + (h - QP), spreads=P - 1 if h == 0 else None)
                    loop_units(1, P, new_h=True)
            unit(L_UNITS, 0, turn=L_TURNS, spreads=NC - 1)
            pe.reg_mov(u_reg, L_UNITS + 1)
            loop_units(1, NC, new_h=True)
            next_unit(0, turn=L_TURNS + 1, finish=0)
            loop_units(1, NC)
            with pe.Fori(1, NC - 1) as P:
                for h in range(QP):
                    next_unit(P, turn=P * QP + (h + L_TURNS), finish=P * QP + (h - 1))
                    loop_units(P + 1, NC)
            for h in range(QP):
                R = NQ - QP + h
                unit(UNITS - QP + h, NC - 1, turn=L_TURNS + R, finish=R - 1)
            for s in range(S):
                turn_total(NQ - 1, s)
                times_w(NQ - 1, s)

        @block.scalar
        def _(act):
            def upper(u, k):
                g = u * G + k
                s, half = k // HC, k % HC
                if half == 0:
                    act.wait_ge(tt_ready, u * S + (s + 1))
                if not (isinstance(u, int) and u == 0 and k < 4):
                    act.wait_ge(pieces_used, g - 3)
                nc.scalar.activation(hi[:, k % 4, :], tt[:, s % 2, half * 4 * T:(half + 1) * 4 * T], ACT.Copy
                                     ).then_inc(hi_ready, 1)

            def sum_m(h, c, s):
                for b_ in range(Q):
                    at = bass.ds((s * Q + b_) * NC + c, 1)
                    last = nc.scalar.activation(mt[:, s, b_ * RUN:(b_ + 1) * RUN], mt[:, s, b_ * RUN:(b_ + 1) * RUN], ACT.Copy,
                                                accum_out=lsum[:, h, at])
                last.then_inc(m_summed, 1)

            def sum_d(h, i, d, s):
                act.wait_ge(d_loaded[s], (d + 1) * 16)
                at = bass.ds(s * NC + (NC - 1) - i, 1)
                nc.scalar.activation(dt_[:, s, :], dt_[:, s, :], ACT.Copy, accum_out=dsum[:, h, at]
                                     ).then_inc(d_summed, 1)

            def relu(P):
                act.wait_ge(nx_scaled, (P + 1) * M)
                nc.scalar.activation(nx[:, :, :], nx[:, :, :], ACT.Relu).then_inc(nx_ready, 1)

            def hs_upper(P, m):
                if m == 0:
                    act.wait_ge(disx_ready, (P + 1) * Q)
                    act.wait_ge(nx_ready, P + 1)
                nc.scalar.activation(hs[:, bass.ds(P * M + m, 1), 0:FD], nx[:, m:m + 1, :], ACT.Copy,
                                     scale=disx[:, m:m + 1]).then_inc(hs_hi, 1)

            def copy_total(n, s):
                act.wait_ge(tot_used, n * S + (s + 1))
                nc.scalar.activation(totT[:, :, :], fin_t[:, 0:FD], ACT.Copy).then_inc(totT_ready, 1)

            def scale_rows(n, s):
                act.wait_ge(fin_ready, n * S + (s + 1))
                nc.scalar.activation(res[:, s, :], fin_o[:, 0:FD], ACT.Copy, scale=dis[:, bass.ds(n * S + s, 1)]
                                     ).then_inc(res_ready, 1)

            HS_AFTER = {4: (0, 1, 2), 5: (3, 4, 5), 6: (6, 7)}

            def unit(u, h=None, c=None, i=None, d=None, finish=None, builds=None, norms=None):
                for k in range(G):
                    upper(u, k)
                    if builds is not None:
                        for m in HS_AFTER.get(k, ()):
                            hs_upper(builds, m)
                    if finish is not None and 3 <= k <= 6:
                        if k > 3:
                            scale_rows(finish, k - 4)
                        copy_total(finish, k - 3)
                    if finish is not None and k == 7:
                        scale_rows(finish, S - 1)
                    if k % HC == HC - 1:
                        s = k // HC
                        if c is not None and s < ACT_SUMS:
                            sum_m(h, c, s)
                        if d is not None:
                            sum_d(h, i, d, s)
                if norms is not None:
                    relu(norms)

            u_reg = counted(act, "act_u", QP)
            d_reg = counted(act, "act_d", NC)

            def next_both(h, i, u=None, **kw):
                unit(act.snap(u_reg) if u is None else u, h=h, c=i, i=i, d=act.snap(d_reg), **kw)
                if u is None:
                    act.reg_add(u_reg, u_reg, 1)
                act.reg_add(d_reg, d_reg, 1)

            def loop_both(h, first, end):
                with act.Fori(first, end) as i:
                    next_both(h, i)

            def loop_only_d(h, first, end):
                with act.Fori(first, end) as i:
                    for s in range(S):
                        sum_d(h, i, act.snap(d_reg), s)
                    act.reg_add(d_reg, d_reg, 1)

            def loop_only_m(first, end, h=None):
                with act.Fori(first, end) as c:
                    unit(act.snap(u_reg), h=h, c=c if h is not None else None)
                    act.reg_add(u_reg, u_reg, 1)

            def sums_free(R):
                act.wait_ge(dsum_clear, R - 1)

            act.wait_ge(fills_ready, FILLS)
            for h in range(QP):
                for i in range(NC // 2):
                    for s in range(S):
                        sum_d(h, i, h * (NC // 2) + i, s)
                if h == 0:
                    relu(0)
                    act.wait_ge(wT_psum, 1)
                    nc.scalar.activation(wT[:, :, :], fin_t[:, :], ACT.Copy).then_inc(wT_ready, 1)
            for m in range(M):
                hs_upper(0, m)
            for h in range(QP):
                sums_free(QP + h)
                next_both(h, 0, u=h, norms=1 if h == 1 else None)
                loop_only_d(h, 1, NC - 1)
            with act.Fori(2, NC // 2) as P:
                for h in range(QP):
                    sums_free(P * QP + h)
                    next_both(h, 0, builds=P - 1 if h == 0 else None, norms=P if h == 1 else None)
                    loop_both(h, 1, P)
                    loop_only_d(h, P, NC - P)
            P = NC // 2
            for h in range(QP):
                sums_free(P * QP + h)
                next_both(h, 0, builds=P - 1 if h == 0 else None, norms=P if h == 1 else None)
                loop_both(h, 1, P)
            with act.Fori(NC // 2 + 1, NC - 1) as P:
                for h in range(QP):
                    sums_free(P * QP + h)
                    next_both(h, 0, builds=P - 1 if h == 0 else None, norms=P if h == 1 else None)
                    loop_both(h, 1, NC - P)
                    loop_only_m(NC - P, P, h)
            P = NC - 1
            for h in range(QP):
                sums_free(P * QP + h)
                next_both(h, 0, builds=P - 1 if h == 0 else None, norms=P if h == 1 else None)
                loop_only_m(1, P, h)

            unit(L_UNITS, builds=NC - 1)
            act.reg_mov(u_reg, L_UNITS + 1)

            def next_unit(**kw):
                unit(act.snap(u_reg), **kw)
                act.reg_add(u_reg, u_reg, 1)

            loop_only_m(1, NC)
            next_unit(finish=0)
            loop_only_m(1, NC)
            with act.Fori(1, NC - 1) as P:
                for h in range(QP):
                    next_unit(finish=P * QP + (h - 1))
                    loop_only_m(P + 1, NC)
            for h in range(QP):
                unit(UNITS - QP + h, finish=NQ - QP + h - 1)
            for s in range(S):
                copy_total(NQ - 1, s)
                scale_rows(NQ - 1, s)

        @block.vector
        def _(dve):
            def turn_slot(u, s):
                if s % V == 0:
                    dve.wait_ge(m_loaded[s // V], (u + 1) * (16 * Q))
                nc.vector.transpose(tt[:, s % 2, :].rearrange("p (m b i) -> p b m i", m=M, b=Q),
                                    mt[:, s, :].rearrange("p (b m j) -> p b m j", b=Q, m=M)).then_inc(tt_ready, 1)

            def lower(u, k):
                s, half = k // HC, k % HC
                dve.wait_ge(hi_ready, u * G + (k + 1))
                nc.vector.tensor_tensor(lo[:, k % 4, :], tt[:, s % 2, half * 4 * T:(half + 1) * 4 * T],
                                        hi[:, k % 4, :].bitcast(F32), ALU.subtract).then_inc(lo_ready, 1)

            def sum_m(h, c, s):
                nc.vector.tensor_reduce(
                    lsum[:, h, :].rearrange("p (s c) -> p s c", c=NC)[:, s * Q:(s + 1) * Q, bass.ds(c, 1)],
                    mt[:, s, :].rearrange("p (b l) -> p b l", b=Q), AX_X, ALU.add).then_inc(m_summed_dve, 1)

            def read_acc(turn, u, s, dst, other):
                dve.wait_ge(pieces_used, u * G + HC * (s + 1))
                if other is None:
                    nc.vector.tensor_copy(dst, acc[s][:, 0:FD]).then_inc(acc_read, 1)
                else:
                    nc.vector.tensor_tensor(dst, acc[s][:, 0:FD], other, ALU.add).then_inc(acc_read, 1)

            def spill(turn, u, s):
                if not (isinstance(turn, int) and turn == 0):
                    dve.wait_ge(part_stored, turn * 16)
                read_acc(turn, u, s, part[:, s, :], None)

            def full(n, u, s):
                dve.wait_ge(tot_loaded, (n + 1) * 16)
                read_acc(n + L_TURNS, u, s, tot[:, s, :], tot[:, s, :])

            def quad_sums(R, h, u, d):
                dve.wait_ge(d_summed, d * S)
                if u is not None:
                    dve.wait_ge(m_summed, u * ACT_SUMS)
                    dve.wait_ge(m_summed_dve, u)
                nc.vector.tensor_reduce(z[:, h, :], lsum[:, h, :].rearrange("p (s c) -> p s c", c=NC),
                                        AX_X, ALU.add).then_inc(quad_summed, 1)
                nc.vector.tensor_reduce(dq[:, h, :], dsum[:, h, :].rearrange("p (s c) -> p s c", c=NC),
                                        AX_X, ALU.add).then_inc(quad_summed, 1)
                dve.wait_ge(quad_summed, (R + 1) * 2)
                for b_ in range(Q):
                    p = slice(b_ * B, (b_ + 1) * B)
                    zb = z[p, h, :].rearrange("p (s b) -> p s b", b=Q)[:, :, b_]
                    nc.vector.tensor_tensor(zb, zb, dq[p, h, :], ALU.add).then_inc(z_ready, 1)
                nc.vector.memset(dsum[:, h, :], 0.0).then_inc(dsum_clear, 1)

            def x_stats(P, ms):
                for m in ms:
                    if m == 0:
                        dve.wait_ge(nx_loaded, (P + 1) * (16 * Q))
                    nc.vector.bn_stats(stats[:, m, :], nx[:, m, :]).then_inc(stats_done, 1)

            def x_aggr(P):
                for m in range(M):
                    nc.vector.bn_aggr(mv[:, m, :], stats[:, m, :]).then_inc(mv_done, 1)

            def x_var(P):
                dve.wait_ge(mv_done, (P + 1) * M)
                nc.vector.tensor_scalar(vare[:, :], mv[:, :, 1], LN_EPS, None, ALU.add).then_inc(vare_ready, 1)

            def x_scale(P, ms):
                for m in ms:
                    if m == 0:
                        dve.wait_ge(rstd_ready, P + 1)
                    nc.vector.tensor_scalar(nx[:, m, :], nx[:, m, :], mv[:, m, 0:1], rstd[:, m:m + 1],
                                            ALU.subtract, ALU.mult).then_inc(nx_scaled, 1)

            def deg_eps(P):
                dve.wait_ge(spread_ready, P + 1)
                nc.vector.tensor_scalar(dege[:, :], deg_ps[:, 0:QP * S * Q], DEG_EPS, None, ALU.add
                                        ).then_inc(dege_ready, 1)

            def place_dis(P):
                dve.wait_ge(disq_ready, P + 1)
                for a in range(Q):
                    p = slice(a * B, (a + 1) * B)
                    nc.vector.tensor_copy(disx[p, :], disq[p, a * M:(a + 1) * M]).then_inc(disx_ready, 1)
                for b_ in range(Q):
                    p = slice(b_ * B, (b_ + 1) * B)
                    nc.vector.tensor_copy(dis[p, bass.ds(P * (QP * S), QP * S)],
                                          disq[p, :].rearrange("p (r b) -> p r b", b=Q)[:, :, b_]
                                          ).then_inc(dis_ready, 1)

            def hs_lower(P, ms):
                for m in ms:
                    dve.wait_ge(hs_hi, P * M + (m + 1))
                    tile = bass.ds(P * M + m, 1)
                    nc.vector.scalar_tensor_tensor(out=hs[:, tile, FD:2 * FD], in0=nx[:, m:m + 1, :],
                                                   scalar=disx[:, m:m + 1], in1=hs[:, tile, 0:FD].bitcast(F32),
                                                   op0=ALU.mult, op1=ALU.subtract).then_inc(hs_ready, 1)

            READ_AT = [0, 1, 2, 4]
            HS_AFTER = {5: (0, 1, 2), 6: (3, 4, 5), 7: (6, 7)}

            def unit(u, h=None, c=None, spills=None, finish=None, builds=None, norms=None, ends=False):
                for k in range(G):
                    if k in READ_AT:
                        s = READ_AT.index(k)
                        if spills is not None:
                            spill(spills, u - 1, s)
                        if finish is not None:
                            full(finish, u - 1, s)
                    if norms is not None and k == 2:
                        dve.wait_ge(stats_done, (norms + 1) * M)
                    lower(u, k)
                    if norms is not None and 5 <= k <= 6:
                        x_scale(norms, range((k - 5) * M // 2, (k - 4) * M // 2))
                    if k % HC == 0 and not (ends and k + HC == G):
                        if not (isinstance(u, int) and u == 0 and k == 0):
                            dve.wait_ge(lo_ready, u * G + k)
                        turn_slot(u, k // HC + 1) if k + HC < G else turn_slot(u + 1, 0)
                    if c is not None and k == G - 2:
                        sum_m(h, c, S - 1)
                    if norms is not None:
                        if k < 2:
                            x_stats(norms, range(k * M // 2, (k + 1) * M // 2))
                        if k == 2:
                            x_aggr(norms)
                        if k == 3:
                            x_var(norms)
                    if builds is not None:
                        if k == 2:
                            deg_eps(builds)
                        if k == 3:
                            place_dis(builds)
                        hs_lower(builds, HS_AFTER.get(k, ()))

            u_reg = counted(dve, "dve_u", QP)
            d_reg = counted(dve, "dve_d", NC + QP * (NC - 1))

            def next_unit(**kw):
                unit(dve.snap(u_reg), **kw)
                dve.reg_add(u_reg, u_reg, 1)

            def loop_units(first, end, h=None):
                with dve.Fori(first, end) as c:
                    next_unit(h=h, c=c if h is not None else None)

            dve.wait_ge(fills_ready, FILLS)
            for h in range(QP):
                for i in range(NC // 2):
                    for s in range(S):
                        t = h * (NC // 2) + i
                        dve.wait_ge(p0_loaded[s], (t + 1) * 16)
                        nc.vector.tensor_reduce(dsum[:, h, s * NC + i:s * NC + i + 1], mt[:, s, :], AX_X, ALU.add
                                                ).then_inc(p0_summed, 1)
                if h == 0:
                    x_stats(0, range(M))
                    dve.wait_ge(stats_done, M)
                    x_aggr(0)
                    x_var(0)
                    x_scale(0, range(M))
                dve.wait_ge(p0_summed, (h + 1) * (NC // 2) * S)
                quad_sums(h, h, None, (h + 1) * (NC // 2))
            deg_eps(0)
            place_dis(0)
            hs_lower(0, range(M))
            turn_slot(0, 0)
            for h in range(QP):
                unit(h, h=h, c=0, spills=0 if h else None, norms=1 if h else None)
                quad_sums(QP + h, h, h + 1, NC + (NC - 1) * (h + 1))
            with dve.Fori(2, NC) as P:
                for h in range(QP):
                    next_unit(h=h, c=0, spills=P * QP + (h - QP - 1), builds=P - 1 if h == 0 else None,
                              norms=P if h == 1 else None)
                    loop_units(1, P, h)
                    with dve.Fori(P, NC) as i:
                        dve.reg_add(d_reg, d_reg, 1)
                    quad_sums(P * QP + h, h, dve.snap(u_reg), dve.snap(d_reg))
            unit(L_UNITS, spills=L_TURNS - 1, builds=NC - 1)
            dve.reg_mov(u_reg, L_UNITS + 1)
            loop_units(1, NC)
            dve.wait_ge(dis_ready, NC * Q)
            next_unit(finish=0)
            loop_units(1, NC)
            with dve.Fori(1, NC - 1) as P:
                for h in range(QP):
                    next_unit(finish=P * QP + (h - 1))
                    loop_units(P + 1, NC)
            for h in range(QP):
                unit(UNITS - QP + h, finish=NQ - QP + h - 1, ends=(h == QP - 1))
            for s in range(S):
                full(NQ - 1, UNITS - 1, s)

        @block.gpsimd
        def _(pool):
            def load_nx(P):
                if not (isinstance(P, int) and P == 0):
                    pool.wait_ge(hs_ready, P * M)
                for a in range(Q):
                    pool.dma_start(nx[a * B:(a + 1) * B, :, :],
                                   x_cols[bass.ds(P, 1), a].rearrange("c j m f -> (c j) m f")
                                   ).then_inc(nx_loaded, 16)

            def power_var(P):
                pool.wait_ge(vare_ready, P + 1)
                nc.gpsimd.tensor_tensor(rstd[:, :], vare[:, :], mhalf[:, 0:M], ALU.pow).then_inc(rstd_ready, 1)

            def power_deg(P):
                pool.wait_ge(dege_ready, P + 1)
                nc.gpsimd.tensor_tensor(disq[:, :], dege[:, :], mhalf[:, :], ALU.pow).then_inc(disq_ready, 1)

            def store_part(R):
                pool.wait_ge(acc_read, (R - (QP - 1)) * S)
                pool.dma_start(part_dram[:, bass.ds(R * S, S), :], part[:, :, :]).then_inc(part_stored, 16)

            def load_last(n):
                if not (isinstance(n, int) and n == 0):
                    pool.wait_ge(tot_used, n * S)
                    pool.wait_ge(o_stored, n * 16)
                pool.dma_start(tot, part_dram[:, bass.ds(n * S, S), :]).then_inc(tot_loaded, 16)
                pool.dma_start(xb, x_rows[:, bass.ds(n * S, S), :]).then_inc(xb_loaded, 16)
                pool.wait_ge(xb_loaded, (n + 1) * 16)
                nc.gpsimd.tensor_tensor(xb, xb, b_bc[:, :].rearrange("p (s f) -> p s f", s=1).to_broadcast([T, S, FD]),
                                        ALU.add).then_inc(xb_ready, 1)

            def store_out(n):
                pool.wait_ge(xb_ready, n + 1)
                pool.wait_ge(res_ready, n * S + S)
                nc.gpsimd.tensor_tensor(xb, xb, res, ALU.add).then_inc(o_ready, 1)
                pool.wait_ge(o_ready, n + 1)
                if isinstance(n, int):
                    rows = n * S
                else:
                    pool.reg_add(out_reg, out_reg, S)
                    rows = pool.snap(out_reg, min_val=S, max_val=(NQ - 1) * S)
                pool.dma_start(out_rows[:, bass.ds(rows, S), :], xb).then_inc(o_stored, 16)

            load_nx(0)
            pool.dma_start(w_sb[:, :, :], W.rearrange("(q p) f -> p q f", p=T)).then_inc(w_loaded, 16)
            pool.dma_start(b_bc[:, :], b.partition_broadcast(T)).then_inc(b_loaded, 16)
            nc.gpsimd.memset(lsum[:, :, :], 0.0).then_inc(fills_ready, 1)
            nc.gpsimd.memset(dsum[:, :, :], 0.0).then_inc(fills_ready, 1)
            nc.gpsimd.memset(mhalf[:, :], -0.5).then_inc(fills_ready, 1)
            nc.gpsimd.memset(zeros[:, :].bitcast(F32), 0.0).then_inc(fills_ready, 1)
            nc.gpsimd.memset(part[:, :, :], 0.0).then_inc(fills_ready, 1)
            nc.gpsimd.memset(ident[:, :], 0.0).then_inc(ident_ready, 1)
            nc.gpsimd.memset(same[:, :], 0.0).then_inc(same_ready, 1)
            pool.wait_ge(ident_ready, 1)
            nc.gpsimd.affine_select(out=ident[:, :], in_=ident[:, :], compare_op=ALU.not_equal, fill=1.0, base=0,
                                    pattern=[[-1, T]], channel_multiplier=1).then_inc(ident_ready, 1)
            for n, off in enumerate(range(-(Q - 1), Q)):
                pool.wait_ge(same_ready, n + 1)
                nc.gpsimd.affine_select(out=same[:, :], in_=same[:, :], compare_op=ALU.not_equal, fill=1.0,
                                        base=off * B, pattern=[[-1, T]], channel_multiplier=1
                                        ).then_inc(same_ready, 1)
            pool.wait_ge(fills_ready, FILLS)
            for R in range(QP):
                pool.dma_start(part_dram[:, R * S:(R + 1) * S, :], part[:, :, :]).then_inc(zero_stored, 16)
            pool.wait_ge(zero_stored, 16 * QP)
            power_var(0)
            power_deg(0)
            load_nx(1)
            power_var(1)
            store_part(QP)
            with pool.Fori(2, NC) as P:
                power_deg(P - 1)
                store_part(P * QP - 1)
                load_nx(P)
                power_var(P)
                store_part(P * QP)
            power_deg(NC - 1)
            store_part(NQ - 1)
            pool.wait_ge(part_stored, 16 * (NQ - QP))
            pool.wait_ge(b_loaded, 16)
            pool.wait_ge(d_summed, D_UNITS * S)
            load_last(0)
            store_out(0)
            out_reg = counted(pool, "pool_out", 0)
            with pool.Fori(1, NQ) as n:
                load_last(n)
                store_out(n)
            pool.wait_ge(o_stored, 16 * NQ)


_INS = ["x", "adj", "L0_gnn_W", "L0_gnn_b"]


def kernel(**inputs):
    import numpy as _np
    import concourse.bacc as _bacc
    from concourse import mybir as _mybir
    from concourse.bass_utils import run_bass_kernel_spmd as _run

    nc = _bacc.Bacc("TRN2", target_bir_lowering=False, num_devices=1)
    arrays, args = {}, []
    for name in _INS:
        a = _np.ascontiguousarray(inputs[name])
        arrays[f"in_{name}_dram"] = a
        args.append(nc.dram_tensor(f"in_{name}_dram", a.shape, _mybir.dt.from_np(a.dtype), kind="ExternalInput").ap())
    shape = inputs["x"].shape
    out = nc.dram_tensor("out_0_dram", shape, _mybir.dt.float32, kind="ExternalOutput").ap()
    part = nc.dram_tensor("part_dram", (128, shape[0] // 128, shape[1]), _mybir.dt.float32, kind="Internal").ap()
    gnn_block_kernel(nc, *args, out, part)
    r = _run(nc, [arrays], core_ids=[0])
    return r.results[0]["out_0_dram"]
```

```python
from contextlib import ExitStack

import concourse.bass as bass
from concourse import mybir

F32 = mybir.dt.float32
F32R = mybir.dt.float32r
ALU = mybir.AluOpType
ACT = mybir.ActivationFunctionType
AX_X = mybir.AxisListType.X

LN_EPS = 1e-5
DEG_EPS = 1e-8


def gnn_block_kernel(nc, x, adj, W, b, out, part_dram):
    N, FD = x.shape
    T = 128
    B = 32
    Q = T // B
    S = 4
    V = 2
    UC = 1024
    RUN = UC // Q
    M = UC // T
    NC = N // UC
    HC = 2
    G = S * HC
    NQ = N // (S * T)
    QP = NQ // NC
    FH = FD // T
    ONES = 2

    E = 3

    L_UNITS = QP * NC * (NC - 1) // 2 + QP * E
    UNITS = QP * NC * NC
    L_TURNS = NQ
    E_TURN = QP * (E - 1)
    assert QP == 2 and FH == 2 and NC == 8 and M == HC * 4 and NC // 2 == E + 1
    FIRST_M = NC
    D_UNITS = NC + QP * NC * (NC - 1) // 2

    def counted(eng, name, start):
        reg = eng.alloc_register(name)
        eng.reg_mov(reg, start)
        return reg

    adj_rows = adj.rearrange("(r p) c -> p r c", p=T)
    adj_blocks = adj.rearrange("(r i) (c a l) -> a i r c l", i=B, a=Q, l=RUN)
    x_rows = x.rearrange("(r p) f -> p r f", p=T)
    x_cols = x.rearrange("(c a m j) f -> c a j m f", a=Q, m=M, j=B)
    out_rows = out.rearrange("(r p) f -> p r f", p=T)

    with ExitStack() as ctx:
        def sb(name, shape, dt=F32):
            return ctx.enter_context(nc.sbuf_tensor(name, shape, dt))

        def pb(name, shape):
            return ctx.enter_context(nc.psum_tensor(name, shape, F32))

        def sem(name):
            return ctx.enter_context(nc.semaphore(name))

        hs = sb("hs", [T, NC * M, 2 * FD + ONES], F32R)
        mt = sb("mt", [T, S, UC])
        dt_ = sb("dt_", [T, S, UC])
        tt = sb("tt", [T, 2, UC])
        hi = sb("hi", [T, 4, 4 * T], F32R)
        lo = sb("lo", [T, 4, 4 * T], F32R)
        dsum = sb("dsum", [T, QP, S * NC])
        deg = sb("deg", [T, QP, S])
        z = sb("z", [T, Q, QP * S])
        nx = sb("nx", [T, M, FD])
        part = sb("part", [T, S, FD + ONES])
        b_bc = sb("b_bc", [T, FD])
        w_sb = sb("w_sb", [T, FH, FD])
        wT = sb("wT", [T, FH, FD])
        totT = sb("totT", [T, FH, T])
        ident = sb("ident", [T, T])
        same = sb("same", [T, T])
        zeros = sb("zeros", [T, T], F32R)
        stats = sb("stats", [T, M, 6])
        mv = sb("mv", [T, M, 2])
        vare = sb("vare", [T, M])
        rstd = sb("rstd", [T, M])
        dege = sb("dege", [T, QP * S])
        disq = sb("disq", [T, QP * S])
        mhalf = sb("mhalf", [T, QP * S])
        disx = sb("disx", [T, M])
        dis = sb("dis", [T, NQ * S])
        tot = dt_[:, 0, :].rearrange("p (s f) -> p s f", s=S)
        xb = [dt_[:, v, :].rearrange("p (s f) -> p s f", s=S) for v in (1, 3)]
        res = dt_[:, 2, :].rearrange("p (s f) -> p s f", s=S)

        acc = [pb(f"acc{s}", [T, 512]) for s in range(S)]
        fin_t = pb("fin_t", [T, 512])
        fin_o = pb("fin_o", [T, 512])
        dis_ps = pb("dis_ps", [T, 512])

        m_loaded = [sem(f"m_loaded{v}") for v in range(S // V)]
        p0_loaded = [sem(f"p0_loaded{s}") for s in range(S)]
        d_loaded = [sem(f"d_loaded{s}") for s in range(S)]
        tt_ready = sem("tt_ready")
        hi_ready = sem("hi_ready")
        lo_ready = sem("lo_ready")
        pieces_used = sem("pieces_used")
        p0_summed = sem("p0_summed")
        d_summed = sem("d_summed")
        quad_summed = sem("quad_summed")
        deg_ready = sem("deg_ready")
        dsum_clear = sem("dsum_clear")
        z_ready = sem("z_ready")
        spread_ready = sem("spread_ready")
        dege_ready = sem("dege_ready")
        disq_ready = sem("disq_ready")
        disx_ready = sem("disx_ready")
        dis_ready = sem("dis_ready")
        nx_loaded = sem("nx_loaded")
        stats_done = sem("stats_done")
        mv_done = sem("mv_done")
        vare_ready = sem("vare_ready")
        rstd_ready = sem("rstd_ready")
        nx_scaled = sem("nx_scaled")
        nx_ready = sem("nx_ready")
        hs_hi = sem("hs_hi")
        hs_ready = sem("hs_ready")
        acc_read = sem("acc_read")
        part_stored = sem("part_stored")
        tot_loaded = sem("tot_loaded")
        tot_used = sem("tot_used")
        totT_ready = sem("totT_ready")
        fin_ready = sem("fin_ready")
        xb_loaded = sem("xb_loaded")
        xb_ready = sem("xb_ready")
        res_ready = sem("res_ready")
        o_ready = sem("o_ready")
        o_stored = sem("o_stored")
        w_loaded = sem("w_loaded")
        b_loaded = sem("b_loaded")
        wT_psum = sem("wT_psum")
        wT_ready = sem("wT_ready")
        ident_ready = sem("ident_ready")
        same_ready = sem("same_ready")
        fills_ready = sem("fills_ready")

        SAME_STEPS = 2 * Q
        FILLS = 5

        block = ctx.enter_context(nc.Block())

        @block.sync
        def _(sp):
            def load_p0(R, c, t, s):
                if t > 0:
                    sp.wait_ge(p0_summed, (t - 1) * S + s + 1)
                sp.dma_start(mt[:, s, :], adj_rows[:, R * S + s, c * UC:(c + 1) * UC]).then_inc(p0_loaded[s], 16)

            def load_m(R, c, u1, v):
                src = [adj_blocks[a, :, bass.ds((R * S + v * V) * Q, V * Q), bass.ds(c, 1), :] for a in range(Q)]
                for a in range(Q):
                    sp.compute_val(src[a].offset * 4)
                if u1 is None:
                    sp.wait_ge(p0_summed, (FIRST_M - 1) * S + (v + 1) * V)
                else:
                    turned = sp.compute_val(u1 * S + (v + 1) * V)
                    sp.wait_ge(tt_ready, turned)
                for a in range(Q):
                    sp.dma_start(mt[a * B:(a + 1) * B, v * V:(v + 1) * V, :].rearrange("i s (b l) -> i (s b) l", b=Q),
                                 src[a].rearrange("i r c l -> i (r c) l")).then_inc(m_loaded[v], 16)

            def load_d(R, c, d1, s):
                src = adj_rows[:, bass.ds(R * S + s, 1), bass.ds(c * UC, UC)]
                sp.compute_val(src.offset * 4)
                if d1 is not None:
                    sp.wait_ge(d_summed, d1 * S + (s + 1))
                sp.dma_start(dt_[:, s:s + 1, :], src).then_inc(d_loaded[s], 16)

            def both(R, i, u1, d1, Rm=None, c=None):
                for v in range(S // V):
                    load_m(R if Rm is None else Rm, i if c is None else c, u1, v)
                    for s in range(v * V, (v + 1) * V):
                        load_d(R, NC - 1 - i, d1, s)

            u_reg = counted(sp, "sp_u", 0)
            d_reg = counted(sp, "sp_d", NC - 1)

            def loop_both(R, first, end):
                with sp.Fori(first, end) as i:
                    both(R, i, sp.snap(u_reg), sp.snap(d_reg))
                    sp.reg_add(u_reg, u_reg, 1)
                    sp.reg_add(d_reg, d_reg, 1)

            def loop_only_d(R, first, end):
                with sp.Fori(first, end) as i:
                    for s in range(S):
                        load_d(R, NC - 1 - i, sp.snap(d_reg), s)
                    sp.reg_add(d_reg, d_reg, 1)

            def loop_only_m(R, first, end):
                with sp.Fori(first, end) as c:
                    for v in range(S // V):
                        load_m(R, c, sp.snap(u_reg), v)
                    sp.reg_add(u_reg, u_reg, 1)

            for R in range(QP):
                for i in range(NC // 2):
                    t = R * (NC // 2) + i
                    for s in range(S):
                        load_d(R, NC - 1 - i, t - 1 if t > 0 else None, s)
                        load_p0(R, i, t, s)
            both(QP, 0, None, NC - 1)
            sp.reg_add(d_reg, d_reg, 1)
            loop_only_d(QP, 1, NC - 1)
            loop_both(QP + 1, 0, 1)
            loop_only_d(QP + 1, 1, NC - 1)
            with sp.Fori(0, QP) as h:
                loop_both(QP * 2 + h, 0, 2)
                loop_only_d(QP * 2 + h, 2, NC - 2)
            with sp.Fori(0, QP) as h:
                loop_both(E * QP + h, 0, E)
                with sp.Fori(0, NC - 2 * E) as c:
                    both(E * QP + h, c + E, sp.snap(u_reg), sp.snap(d_reg), Rm=h, c=c)
                    sp.reg_add(u_reg, u_reg, 1)
                    sp.reg_add(d_reg, d_reg, 1)
                loop_only_m(h, NC - 2 * E, E)
            with sp.Fori(0, QP) as h:
                loop_both(NC // 2 * QP + h, 0, NC // 2)
            with sp.Fori(NC // 2 + 1, NC) as P:
                with sp.Fori(0, QP) as h:
                    loop_both(P * QP + h, 0, NC - P)
                    loop_only_m(P * QP + h, NC - P, P)
            for v in range(S // V):
                load_m(0, E, L_UNITS - 1, v)
            sp.reg_mov(u_reg, L_UNITS)
            loop_only_m(0, E + 1, NC)
            loop_only_m(1, E, NC)
            with sp.Fori(1, NC) as P:
                with sp.Fori(0, QP) as h:
                    loop_only_m(P * QP + h, P, NC)

        @block.tensor
        def _(pe):
            def products(u, c, k, sums):
                s, half = k // HC, k % HC
                end = 2 * FD + (ONES if sums else 0)
                pe.wait_ge(lo_ready, u * G + (k + 1))
                for j in range(4):
                    tile = bass.ds(c * M + (half * 4 + j), 1)
                    for piece, cols in ((hi, (0, FD)), (hi, (FD, end)), (lo, (FD, end))):
                        last = pe.matmul(acc[s][:, 0:cols[1] - cols[0]], piece[:, k % 4, j * T:(j + 1) * T],
                                         hs[:, tile, cols[0]:cols[1]], start=False, stop=True, skip_group_check=True)
                last.then_inc(pieces_used, 1)

            def clear(turn, s):
                if not (isinstance(turn, int) and turn == 0):
                    pe.wait_ge(acc_read, (turn - 1) * S + (s + 1))
                pe.matmul(acc[s][:, 0:2], zeros[:, :], zeros[:, 0:2], start=True, stop=True, skip_group_check=True)

            def spread(P):
                pe.wait_ge(z_ready, (P + 1) * Q)
                pe.matmul(dis_ps[:, 0:QP * S * Q], same[:, :], z[:, :, :], start=True, stop=True
                          ).then_inc(spread_ready, 1)

            def turn_total(n, s):
                pe.wait_ge(acc_read, (n + L_TURNS) * S + (s + 1))
                for f in range(FH):
                    last = pe.transpose(fin_t[:, f * T:(f + 1) * T], tot[:, s, f * T:(f + 1) * T], ident[:, :])
                last.then_inc(tot_used, 1)

            def times_w(n, s):
                pe.wait_ge(totT_ready, n * S + (s + 1))
                for f in range(FH):
                    last = pe.matmul(fin_o[:, 0:FD], totT[:, f, :], wT[:, f, :], start=(f == 0), stop=(f == FH - 1))
                last.then_inc(fin_ready, 1)

            def unit(u, c, turn=None, finish=None, spreads=None, new_h=False, sums=False):
                if new_h:
                    pe.wait_ge(hs_ready, (c + 1) * M)
                for k in range(G):
                    if turn is not None and k % HC == 0:
                        clear(turn, k // HC)
                    products(u, c, k, sums)
                    if spreads is not None and k == 2:
                        spread(spreads)
                    if finish is not None:
                        if 2 <= k <= 5:
                            times_w(finish, k - 2)
                        if 1 <= k <= 4:
                            turn_total(finish, k - 1)

            pe.wait_ge(ident_ready, 2)
            pe.wait_ge(same_ready, SAME_STEPS)
            pe.wait_ge(fills_ready, FILLS)
            pe.wait_ge(w_loaded, 16)
            for f in range(FH):
                for o in range(FH):
                    last = pe.transpose(fin_t[:, (f * FH + o) * T:(f * FH + o + 1) * T],
                                        w_sb[:, o, f * T:(f + 1) * T], ident[:, :])
            last.then_inc(wT_psum, 1)
            pe.wait_ge(wT_ready, 1)

            spread(0)
            for h in range(QP):
                unit(h, 0, turn=h, new_h=True, sums=True)
            u_reg = counted(pe, "pe_u", QP)

            def next_unit(c, **kw):
                unit(pe.snap(u_reg), c, **kw)
                pe.reg_add(u_reg, u_reg, 1)

            def loop_units(first, end, **kw):
                with pe.Fori(first, end) as c:
                    next_unit(c, **kw)

            for h in range(QP):
                next_unit(0, turn=QP + h, spreads=1 if h == 0 else None, sums=True)
                next_unit(1, new_h=True, sums=True)
            for h in range(QP):
                next_unit(0, turn=E_TURN + 2 * h, spreads=E - 1 if h == 0 else None, sums=True)
                loop_units(1, E, new_h=True, sums=True)
                next_unit(0, turn=E_TURN + 2 * h + 1, sums=True)
                loop_units(1, E, sums=True)
            with pe.Fori(E + 1, NC) as P:
                for h in range(QP):
                    next_unit(0, turn=P * QP + h, spreads=P - 1 if h == 0 else None, sums=True)
                    loop_units(1, P, new_h=True, sums=True)
            unit(L_UNITS, E, turn=L_TURNS, spreads=NC - 1)
            pe.reg_mov(u_reg, L_UNITS + 1)
            loop_units(E + 1, NC, new_h=True)
            next_unit(E, turn=L_TURNS + 1, finish=0)
            loop_units(E + 1, NC)
            with pe.Fori(1, NC - 1) as P:
                for h in range(QP):
                    next_unit(P, turn=P * QP + (h + L_TURNS), finish=P * QP + (h - 1))
                    loop_units(P + 1, NC)
            for h in range(QP):
                R = NQ - QP + h
                unit(UNITS - QP + h, NC - 1, turn=L_TURNS + R, finish=R - 1)
            for s in range(S):
                turn_total(NQ - 1, s)
                times_w(NQ - 1, s)

        @block.scalar
        def _(act):
            def upper(u, k):
                g = u * G + k
                s, half = k // HC, k % HC
                if half == 0:
                    act.wait_ge(tt_ready, u * S + (s + 1))
                if not (isinstance(u, int) and u == 0 and k < 4):
                    act.wait_ge(pieces_used, g - 3)
                nc.scalar.activation(hi[:, k % 4, :], tt[:, s % 2, half * 4 * T:(half + 1) * 4 * T], ACT.Copy
                                     ).then_inc(hi_ready, 1)

            def sum_d(h, i, d, s):
                act.wait_ge(d_loaded[s], (d + 1) * 16)
                at = bass.ds(s * NC + (NC - 1) - i, 1)
                nc.scalar.activation(dt_[:, s, :], dt_[:, s, :], ACT.Copy, accum_out=dsum[:, h, at]
                                     ).then_inc(d_summed, 1)

            def relu(P):
                act.wait_ge(nx_scaled, (P + 1) * M)
                nc.scalar.activation(nx[:, :, :], nx[:, :, :], ACT.Relu).then_inc(nx_ready, 1)

            def hs_upper(P, m):
                if m == 0:
                    act.wait_ge(disx_ready, (P + 1) * Q)
                    act.wait_ge(nx_ready, P + 1)
                nc.scalar.activation(hs[:, bass.ds(P * M + m, 1), FD:2 * FD], nx[:, m:m + 1, :], ACT.Copy,
                                     scale=disx[:, m:m + 1]).then_inc(hs_hi, 1)

            def copy_total(n, s):
                act.wait_ge(tot_used, n * S + (s + 1))
                nc.scalar.activation(totT[:, :, :], fin_t[:, 0:FD], ACT.Copy).then_inc(totT_ready, 1)

            def scale_rows(n, s):
                act.wait_ge(fin_ready, n * S + (s + 1))
                if s == 0 and not (isinstance(n, int) and n == 0):
                    act.wait_ge(o_ready, n)
                nc.scalar.activation(res[:, s, :], fin_o[:, 0:FD], ACT.Copy, scale=dis[:, bass.ds(n * S + s, 1)]
                                     ).then_inc(res_ready, 1)

            def spill(turn, u, s, taken):
                if s == 0 and not (isinstance(turn, int) and turn == 0):
                    act.wait_ge(part_stored, turn * 16)
                    act.wait_ge(deg_ready, taken)
                act.wait_ge(pieces_used, u * G + HC * (s + 1))
                nc.scalar.activation(part[:, s, :], acc[s][:, 0:FD + ONES], ACT.Copy).then_inc(acc_read, 1)

            READ_AT = [0, 0, 2, 4]
            HS_AFTER = {6: (0, 1, 2), 7: range(3, M)}

            def unit(u, h=None, i=None, d=None, spills=None, taken=None, finish=None, builds=None,
                     norms=None):
                for k in range(G):
                    if spills is not None:
                        for s in range(S):
                            if READ_AT[s] == k:
                                spill(spills, u - 1, s, spills if taken is None else taken)
                    upper(u, k)
                    if builds is not None:
                        for m in HS_AFTER.get(k, ()):
                            hs_upper(builds, m)
                    if finish is not None and 3 <= k <= 6:
                        if k > 3:
                            scale_rows(finish, k - 4)
                        copy_total(finish, k - 3)
                    if finish is not None and k == 7:
                        scale_rows(finish, S - 1)
                    if k % HC == HC - 1:
                        s = k // HC
                        if d is not None:
                            sum_d(h, i, d, s)
                if norms is not None:
                    relu(norms)

            u_reg = counted(act, "act_u", QP)
            d_reg = counted(act, "act_d", NC)

            def next_both(h, i, u=None, **kw):
                unit(act.snap(u_reg) if u is None else u, h=h, i=i, d=act.snap(d_reg), **kw)
                if u is None:
                    act.reg_add(u_reg, u_reg, 1)
                act.reg_add(d_reg, d_reg, 1)

            def loop_both(h, first, end):
                with act.Fori(first, end) as i:
                    next_both(h, i)

            def loop_only_d(h, first, end):
                with act.Fori(first, end) as i:
                    for s in range(S):
                        sum_d(h, i, act.snap(d_reg), s)
                    act.reg_add(d_reg, d_reg, 1)

            def loop_only_m(first, end):
                with act.Fori(first, end) as _:
                    unit(act.snap(u_reg))
                    act.reg_add(u_reg, u_reg, 1)

            def sums_free(R):
                act.wait_ge(dsum_clear, R - 1)

            def start_quad(P, h):
                after_e = isinstance(P, int) and P == E + 1 and h == 0
                next_both(h, 0, spills=P * QP + (h - 1), taken=P * QP + (h - 1 - QP) + (1 if after_e else 0),
                          builds=P - 1 if h == 0 else None, norms=P if h == 1 else None)

            act.wait_ge(fills_ready, FILLS)
            for h in range(QP):
                for i in range(NC // 2):
                    for s in range(S):
                        sum_d(h, i, h * (NC // 2) + i, s)
                if h == 0:
                    relu(0)
                    act.wait_ge(wT_psum, 1)
                    nc.scalar.activation(wT[:, :, :], fin_t[:, :], ACT.Copy).then_inc(wT_ready, 1)
            for m in range(M):
                hs_upper(0, m)
            for h in range(QP):
                sums_free(QP + h)
                next_both(h, 0, u=h, spills=0 if h else None, norms=1 if h == 1 else None)
                loop_only_d(h, 1, NC - 1)
            for h in range(QP):
                sums_free(2 * QP + h)
                next_both(h, 0, spills=QP + h - 1, builds=1 if h == 0 else None, norms=2 if h == 1 else None)
                next_both(h, 1)
                loop_only_d(h, 2, NC - 2)
            for h in range(QP):
                sums_free(E * QP + h)
                next_both(h, 0, spills=E_TURN + 2 * h - 1, builds=E - 1 if h == 0 else None,
                          norms=E if h == 1 else None)
                loop_both(h, 1, E)
                next_both(h, E, spills=E_TURN + 2 * h, taken=E_TURN + h)
                next_both(h, E + 1)
                loop_only_m(2, E)
            P = NC // 2
            for h in range(QP):
                sums_free(P * QP + h)
                start_quad(P, h)
                loop_both(h, 1, P)
            with act.Fori(NC // 2 + 1, NC - 1) as P:
                for h in range(QP):
                    sums_free(P * QP + h)
                    start_quad(P, h)
                    loop_both(h, 1, NC - P)
                    loop_only_m(NC - P, P)
            P = NC - 1
            for h in range(QP):
                sums_free(P * QP + h)
                start_quad(P, h)
                loop_only_m(1, P)

            unit(L_UNITS, spills=L_TURNS - 1, taken=L_TURNS - 1 - QP, builds=NC - 1)
            act.reg_mov(u_reg, L_UNITS + 1)

            def next_unit(**kw):
                unit(act.snap(u_reg), **kw)
                act.reg_add(u_reg, u_reg, 1)

            loop_only_m(E + 1, NC)
            next_unit(finish=0)
            loop_only_m(E + 1, NC)
            with act.Fori(1, NC - 1) as P:
                for h in range(QP):
                    next_unit(finish=P * QP + (h - 1))
                    loop_only_m(P + 1, NC)
            for h in range(QP):
                unit(UNITS - QP + h, finish=NQ - QP + h - 1)
            for s in range(S):
                copy_total(NQ - 1, s)
                scale_rows(NQ - 1, s)

        @block.vector
        def _(dve):
            def turn_slot(u, s):
                if s % V == 0:
                    dve.wait_ge(m_loaded[s // V], (u + 1) * (16 * Q))
                nc.vector.transpose(tt[:, s % 2, :].rearrange("p (m b i) -> p b m i", m=M, b=Q),
                                    mt[:, s, :].rearrange("p (b m j) -> p b m j", b=Q, m=M)).then_inc(tt_ready, 1)

            def lower(u, k):
                s, half = k // HC, k % HC
                dve.wait_ge(hi_ready, u * G + (k + 1))
                nc.vector.tensor_tensor(lo[:, k % 4, :], tt[:, s % 2, half * 4 * T:(half + 1) * 4 * T],
                                        hi[:, k % 4, :].bitcast(F32), ALU.subtract).then_inc(lo_ready, 1)

            def add_sums(turn, R, h):
                dve.wait_ge(acc_read, (turn + 1) * S)
                dve.wait_ge(quad_summed, R + 1)
                nc.vector.tensor_tensor(deg[:, h, :], deg[:, h, :], part[:, :, FD], ALU.add).then_inc(deg_ready, 1)

            def full(n, u, s):
                dve.wait_ge(tot_loaded, (n + 1) * 16)
                dve.wait_ge(pieces_used, u * G + HC * (s + 1))
                nc.vector.tensor_tensor(tot[:, s, :], tot[:, s, :], acc[s][:, 0:FD], ALU.add).then_inc(acc_read, 1)

            def quad_sums(P, h, d):
                if not (isinstance(P, int) and P == 0):
                    dve.wait_ge(dege_ready, P)
                dve.wait_ge(d_summed, d * S)
                nc.vector.tensor_reduce(deg[:, h, :], dsum[:, h, :].rearrange("p (s c) -> p s c", c=NC),
                                        AX_X, ALU.add).then_inc(quad_summed, 1)
                dve.wait_ge(quad_summed, P * QP + (h + 1))
                nc.vector.memset(dsum[:, h, :], 0.0).then_inc(dsum_clear, 1)

            def deg_eps(P):
                if isinstance(P, int) and P == 0:
                    dve.wait_ge(quad_summed, QP)
                else:
                    dve.wait_ge(deg_ready, P * QP)
                nc.vector.tensor_scalar(dege[:, :], deg[:, :, :].rearrange("p h s -> p (h s)"), DEG_EPS, None, ALU.add
                                        ).then_inc(dege_ready, 1)

            def fill_z(P):
                if not (isinstance(P, int) and P == 0):
                    dve.wait_ge(spread_ready, P)
                dve.wait_ge(disq_ready, P + 1)
                for b_ in range(Q):
                    p = slice(b_ * B, (b_ + 1) * B)
                    nc.vector.tensor_copy(z[p, b_, :], disq[p, :]).then_inc(z_ready, 1)
                nc.vector.tensor_copy(dis[:, bass.ds(P * (QP * S), QP * S)], disq[:, :]).then_inc(dis_ready, 1)

            def x_stats(P, ms):
                for m in ms:
                    if m == 0:
                        dve.wait_ge(nx_loaded, (P + 1) * (16 * Q))
                    nc.vector.bn_stats(stats[:, m, :], nx[:, m, :]).then_inc(stats_done, 1)

            def x_aggr(P):
                for m in range(M):
                    nc.vector.bn_aggr(mv[:, m, :], stats[:, m, :]).then_inc(mv_done, 1)

            def x_var(P):
                dve.wait_ge(mv_done, (P + 1) * M)
                nc.vector.tensor_scalar(vare[:, :], mv[:, :, 1], LN_EPS, None, ALU.add).then_inc(vare_ready, 1)

            def x_scale(P, ms):
                for m in ms:
                    if m == 0:
                        dve.wait_ge(rstd_ready, P + 1)
                    nc.vector.tensor_scalar(nx[:, m, :], nx[:, m, :], mv[:, m, 0:1], rstd[:, m:m + 1],
                                            ALU.subtract, ALU.mult).then_inc(nx_scaled, 1)

            def place_dis(P):
                dve.wait_ge(spread_ready, P + 1)
                for a in range(Q):
                    p = slice(a * B, (a + 1) * B)
                    nc.vector.tensor_copy(disx[p, :].rearrange("p (r b) -> p r b", b=Q),
                                          dis_ps[p, 0:Q * QP * S].rearrange("p (b r) -> p r b", b=Q)
                                          [:, a * HC:(a + 1) * HC, :]).then_inc(disx_ready, 1)

            def hs_lower(P, ms):
                for m in ms:
                    dve.wait_ge(hs_hi, P * M + (m + 1))
                    tile = bass.ds(P * M + m, 1)
                    nc.vector.scalar_tensor_tensor(out=hs[:, tile, 0:FD], in0=nx[:, m:m + 1, :],
                                                   scalar=disx[:, m:m + 1], in1=hs[:, tile, FD:2 * FD].bitcast(F32),
                                                   op0=ALU.mult, op1=ALU.subtract).then_inc(hs_ready, 1)

            READ_AT = [0, 1, 2, 4]
            HS_AFTER = {6: (0, 1, 2), 7: range(3, M)}

            def unit(u, h=None, spills=None, R=None, finish=None, builds=None, norms=None, ends=False):
                for k in range(G):
                    if k in READ_AT:
                        s = READ_AT.index(k)
                        if finish is not None:
                            full(finish, u - 1, s)
                    if norms is not None and k == 2:
                        dve.wait_ge(stats_done, (norms + 1) * M)
                    if spills is not None and k == 4:
                        add_sums(spills, R, h)
                    if builds is not None:
                        if k == 4:
                            deg_eps(builds)
                        if k == 5:
                            fill_z(builds)
                        if k == 6:
                            place_dis(builds)
                    lower(u, k)
                    if norms is not None and 5 <= k <= 6:
                        x_scale(norms, range((k - 5) * M // 2, (k - 4) * M // 2))
                    if k % HC == 0 and not (ends and k + HC == G):
                        if not (isinstance(u, int) and u == 0 and k == 0):
                            dve.wait_ge(lo_ready, u * G + k)
                        turn_slot(u, k // HC + 1) if k + HC < G else turn_slot(u + 1, 0)
                    if norms is not None:
                        if k < 2:
                            x_stats(norms, range(k * M // 2, (k + 1) * M // 2))
                        if k == 2:
                            x_aggr(norms)
                        if k == 3:
                            x_var(norms)
                    if builds is not None:
                        hs_lower(builds, HS_AFTER.get(k, ()))

            u_reg = counted(dve, "dve_u", QP)
            d_reg = counted(dve, "dve_d", NC + QP * sum(NC - P for P in range(1, NC // 2 + 1)))

            def next_unit(**kw):
                unit(dve.snap(u_reg), **kw)
                dve.reg_add(u_reg, u_reg, 1)

            def loop_units(first, end):
                with dve.Fori(first, end) as _:
                    next_unit()

            dve.wait_ge(fills_ready, FILLS)
            for h in range(QP):
                for i in range(NC // 2):
                    for s in range(S):
                        t = h * (NC // 2) + i
                        dve.wait_ge(p0_loaded[s], (t + 1) * 16)
                        nc.vector.tensor_reduce(dsum[:, h, s * NC + i:s * NC + i + 1], mt[:, s, :], AX_X, ALU.add
                                                ).then_inc(p0_summed, 1)
                if h == 0:
                    x_stats(0, range(M))
                    dve.wait_ge(stats_done, M)
                    x_aggr(0)
                    x_var(0)
                    x_scale(0, range(M))
                dve.wait_ge(p0_summed, (h + 1) * (NC // 2) * S)
                quad_sums(0, h, (h + 1) * (NC // 2))
            deg_eps(0)
            fill_z(0)
            place_dis(0)
            hs_lower(0, range(M))
            turn_slot(0, 0)
            for h in range(QP):
                unit(h, h=0, spills=0 if h else None, R=QP, norms=1 if h else None)
                quad_sums(1, h, NC + (NC - 1) * (h + 1))
            for h in range(QP):
                next_unit(h=1 - h, spills=QP + h - 1, R=2 * QP + h - 1, builds=1 if h == 0 else None,
                          norms=2 if h == 1 else None)
                next_unit()
                quad_sums(2, h, NC + QP * (NC - 1) + (h + 1) * (NC - 2))
            for h in range(QP):
                if h == 0:
                    next_unit(h=1, spills=E_TURN - 1, R=E * QP - 1, builds=E - 1)
                else:
                    next_unit(norms=E)
                loop_units(1, E)
                next_unit()
                loop_units(1, E)
                quad_sums(E, h, NC + QP * sum(NC - p for p in range(1, E)) + (h + 1) * (NC - E))
                add_sums(E_TURN + 2 * h, E * QP + h, h)
            P = E + 1
            for h in range(QP):
                if h == 0:
                    next_unit(builds=E)
                else:
                    next_unit(h=0, spills=P * QP, R=P * QP, norms=P)
                loop_units(1, P)
                quad_sums(P, h, NC + QP * sum(NC - p for p in range(1, P)) + (h + 1) * (NC - P))
            with dve.Fori(E + 2, NC) as P:
                for h in range(QP):
                    next_unit(h=1 - h, spills=P * QP + (h - 1), R=P * QP + (h - 1), builds=P - 1 if h == 0 else None,
                              norms=P if h == 1 else None)
                    loop_units(1, P)
                    with dve.Fori(P, NC) as i:
                        dve.reg_add(d_reg, d_reg, 1)
                    quad_sums(P, h, dve.snap(d_reg))
            unit(L_UNITS, h=1, spills=L_TURNS - 1, R=NQ - 1, builds=NC - 1)
            dve.reg_mov(u_reg, L_UNITS + 1)
            loop_units(E + 1, NC)
            dve.wait_ge(dis_ready, NC)
            next_unit(finish=0)
            loop_units(E + 1, NC)
            with dve.Fori(1, NC - 1) as P:
                for h in range(QP):
                    next_unit(finish=P * QP + (h - 1))
                    loop_units(P + 1, NC)
            for h in range(QP):
                unit(UNITS - QP + h, finish=NQ - QP + h - 1, ends=(h == QP - 1))
            for s in range(S):
                full(NQ - 1, UNITS - 1, s)

        @block.gpsimd
        def _(pool):
            def load_nx(P):
                if not (isinstance(P, int) and P == 0):
                    pool.wait_ge(hs_ready, P * M)
                for a in range(Q):
                    pool.dma_start(nx[a * B:(a + 1) * B, :, :],
                                   x_cols[bass.ds(P, 1), a].rearrange("c j m f -> (c j) m f")
                                   ).then_inc(nx_loaded, 16)

            def power_var(P):
                pool.wait_ge(vare_ready, P + 1)
                nc.gpsimd.tensor_tensor(rstd[:, :], vare[:, :], mhalf[:, 0:M], ALU.pow).then_inc(rstd_ready, 1)

            def power_deg(P):
                pool.wait_ge(dege_ready, P + 1)
                nc.gpsimd.tensor_tensor(disq[:, :], dege[:, :], mhalf[:, :], ALU.pow).then_inc(disq_ready, 1)

            def store_part(turn, R):
                pool.wait_ge(acc_read, turn * S + S)
                pool.dma_start(part_dram[:, bass.ds(R * S, S), :], part[:, :, 0:FD]).then_inc(part_stored, 16)

            def load_tot(n):
                if not (isinstance(n, int) and n == 0):
                    pool.wait_ge(tot_used, n * S)
                pool.dma_start(tot, part_dram[:, bass.ds(n * S, S), :]).then_inc(tot_loaded, 16)

            def load_xb(n, v):
                if not (isinstance(n, int) and n < 2):
                    pool.wait_ge(o_stored, (n - 1) * 16)
                pool.dma_start(xb[v], x_rows[:, bass.ds(n * S, S), :]).then_inc(xb_loaded, 16)

            def add_bias(n, v):
                pool.wait_ge(xb_loaded, (n + 1) * 16)
                bias = b_bc[:, :].rearrange("p (s f) -> p s f", s=1).to_broadcast([T, S, FD])
                nc.gpsimd.tensor_tensor(xb[v], xb[v], bias, ALU.add).then_inc(xb_ready, 1)

            def output(n, v):
                pool.wait_ge(xb_ready, n + 1)
                pool.wait_ge(res_ready, n * S + S)
                nc.gpsimd.tensor_tensor(xb[v], xb[v], res, ALU.add).then_inc(o_ready, 1)
                pool.wait_ge(o_ready, n + 1)
                if isinstance(n, int):
                    rows = n * S
                else:
                    pool.reg_add(out_reg, out_reg, S)
                    rows = pool.snap(out_reg, min_val=S, max_val=(NQ - 2) * S)
                pool.dma_start(out_rows[:, bass.ds(rows, S), :], xb[v]).then_inc(o_stored, 16)

            load_nx(0)
            pool.dma_start(w_sb[:, :, :], W.rearrange("(q p) f -> p q f", p=T)).then_inc(w_loaded, 16)
            pool.dma_start(b_bc[:, :], b.partition_broadcast(T)).then_inc(b_loaded, 16)
            nc.gpsimd.memset(z[:, :, :], 0.0).then_inc(fills_ready, 1)
            nc.gpsimd.memset(hs[:, :, 2 * FD:2 * FD + ONES].bitcast(F32), 1.0).then_inc(fills_ready, 1)
            nc.gpsimd.memset(dsum[:, :, :], 0.0).then_inc(fills_ready, 1)
            nc.gpsimd.memset(mhalf[:, :], -0.5).then_inc(fills_ready, 1)
            nc.gpsimd.memset(zeros[:, :].bitcast(F32), 0.0).then_inc(fills_ready, 1)
            nc.gpsimd.memset(ident[:, :], 0.0).then_inc(ident_ready, 1)
            nc.gpsimd.memset(same[:, :], 0.0).then_inc(same_ready, 1)
            pool.wait_ge(ident_ready, 1)
            nc.gpsimd.affine_select(out=ident[:, :], in_=ident[:, :], compare_op=ALU.not_equal, fill=1.0, base=0,
                                    pattern=[[-1, T]], channel_multiplier=1).then_inc(ident_ready, 1)
            for n, off in enumerate(range(-(Q - 1), Q)):
                pool.wait_ge(same_ready, n + 1)
                nc.gpsimd.affine_select(out=same[:, :], in_=same[:, :], compare_op=ALU.not_equal, fill=1.0,
                                        base=off * B, pattern=[[-1, T]], channel_multiplier=1
                                        ).then_inc(same_ready, 1)
            pool.wait_ge(fills_ready, FILLS)
            power_var(0)
            power_deg(0)
            load_nx(1)
            power_var(1)
            store_part(0, QP)
            power_deg(1)
            store_part(1, QP + 1)
            load_nx(2)
            power_var(2)
            store_part(2, QP + 2)
            power_deg(E - 1)
            store_part(E_TURN - 1, E * QP - 1)
            load_nx(E)
            store_part(E_TURN, E * QP)
            power_var(E)
            store_part(E_TURN + 1, 0)
            store_part(E_TURN + 2, E * QP + 1)
            power_deg(E)
            store_part(E_TURN + 3, 1)
            load_nx(E + 1)
            power_var(E + 1)
            store_part(E_TURN + 4, (E + 1) * QP)
            with pool.Fori(E + 2, NC) as P:
                power_deg(P - 1)
                store_part(P * QP - 1, P * QP - 1)
                load_nx(P)
                power_var(P)
                store_part(P * QP, P * QP)
            power_deg(NC - 1)
            store_part(NQ - 1, NQ - 1)
            pool.wait_ge(part_stored, 16 * L_TURNS)
            pool.wait_ge(b_loaded, 16)
            pool.wait_ge(d_summed, D_UNITS * S)
            load_tot(0)
            load_xb(0, 0)
            add_bias(0, 0)
            load_tot(1)
            load_xb(1, 1)
            output(0, 0)
            add_bias(1, 1)
            out_reg = counted(pool, "pool_out", 0)
            with pool.Fori(1, NQ // 2) as w:
                for v in range(2):
                    load_tot(w * 2 + v)
                    load_xb(w * 2 + v, v)
                    output(w * 2 + (v - 1), 1 - v)
                    add_bias(w * 2 + v, v)
            output(NQ - 1, 1)
            pool.wait_ge(o_stored, 16 * NQ)


_INS = ["x", "adj", "L0_gnn_W", "L0_gnn_b"]


def kernel(**inputs):
    import numpy as _np
    import concourse.bacc as _bacc
    from concourse import mybir as _mybir
    from concourse.bass_utils import run_bass_kernel_spmd as _run

    nc = _bacc.Bacc("TRN2", target_bir_lowering=False, num_devices=1)
    arrays, args = {}, []
    for name in _INS:
        a = _np.ascontiguousarray(inputs[name])
        arrays[f"in_{name}_dram"] = a
        args.append(nc.dram_tensor(f"in_{name}_dram", a.shape, _mybir.dt.from_np(a.dtype), kind="ExternalInput").ap())
    shape = inputs["x"].shape
    out = nc.dram_tensor("out_0_dram", shape, _mybir.dt.float32, kind="ExternalOutput").ap()
    part = nc.dram_tensor("part_dram", (128, shape[0] // 128, shape[1]), _mybir.dt.float32, kind="Internal").ap()
    gnn_block_kernel(nc, *args, out, part)
    r = _run(nc, [arrays], core_ids=[0])
    return r.results[0]["out_0_dram"]
```
